# Optimizing a Trainium2 kernel written in Bass

```python
import numpy as np
import jax
import jax.numpy as jnp

def _softmax(x, axis=-1):
    return jax.nn.softmax(x, axis=axis)

def _gelu(x):
    return jax.nn.gelu(x, approximate=True)

def _silu(x):
    return jax.nn.silu(x)

def _sigmoid(x):
    return jax.nn.sigmoid(x)

def _layernorm(x, axis=-1, eps=1e-05):
    m = jnp.mean(x, axis=axis, keepdims=True)
    v = jnp.var(x, axis=axis, keepdims=True)
    return (x - m) / jnp.sqrt(v + eps)

def _scatter_add(tgt, idx, src, axis=0):
    return tgt.at[idx].add(src)

def _segment_sum(src, seg, n):
    return jax.ops.segment_sum(src, seg, n)
kernel_name = 'mk_rec_standalone_d1_rec_r8_65707b'

def setup_inputs(seed: int=0):
    np.random.seed(seed)
    _w = jnp.asarray

    def _rec_inputs():
        import jax
        import jax.numpy as jnp
        _rk = jax.random.key(seed)
        r_numerical_input = -0.00338568 + 1.0005 * jax.random.normal(jax.random.fold_in(_rk, 1), (1024, 13), jnp.float32)
        r_categorical_inputs = jnp.stack([jax.random.randint(jax.random.fold_in(jax.random.fold_in(_rk, 2), 0), (1024,), 2, 12500, jnp.int32), jax.random.randint(jax.random.fold_in(jax.random.fold_in(_rk, 2), 1), (1024,), 1, 99999, jnp.int32), jax.random.randint(jax.random.fold_in(jax.random.fold_in(_rk, 2), 2), (1024,), 0, 12500, jnp.int32), jax.random.randint(jax.random.fold_in(jax.random.fold_in(_rk, 2), 3), (1024,), 5, 12500, jnp.int32), jax.random.randint(jax.random.fold_in(jax.random.fold_in(_rk, 2), 4), (1024,), 20, 99993, jnp.int32), jax.random.randint(jax.random.fold_in(jax.random.fold_in(_rk, 2), 5), (1024,), 0, 99993, jnp.int32), jax.random.randint(jax.random.fold_in(jax.random.fold_in(_rk, 2), 6), (1024,), 2, 99999, jnp.int32), jax.random.randint(jax.random.fold_in(jax.random.fold_in(_rk, 2), 7), (1024,), 2, 99995, jnp.int32), jax.random.randint(jax.random.fold_in(jax.random.fold_in(_rk, 2), 8), (1024,), 0, 99999, jnp.int32), jax.random.randint(jax.random.fold_in(jax.random.fold_in(_rk, 2), 9), (1024,), 2, 99986, jnp.int32), jax.random.randint(jax.random.fold_in(jax.random.fold_in(_rk, 2), 10), (1024,), 4, 99999, jnp.int32), jax.random.randint(jax.random.fold_in(jax.random.fold_in(_rk, 2), 11), (1024,), 15, 99999, jnp.int32), jax.random.randint(jax.random.fold_in(jax.random.fold_in(_rk, 2), 12), (1024,), 0, 99989, jnp.int32), jax.random.randint(jax.random.fold_in(jax.random.fold_in(_rk, 2), 13), (1024,), 5, 99990, jnp.int32), jax.random.randint(jax.random.fold_in(jax.random.fold_in(_rk, 2), 14), (1024,), 2, 99996, jnp.int32), jax.random.randint(jax.random.fold_in(jax.random.fold_in(_rk, 2), 15), (1024,), 3, 99994, jnp.int32), jax.random.randint(jax.random.fold_in(jax.random.fold_in(_rk, 2), 16), (1024,), 0, 99998, jnp.int32), jax.random.randint(jax.random.fold_in(jax.random.fold_in(_rk, 2), 17), (1024,), 13, 99998, jnp.int32), jax.random.randint(jax.random.fold_in(jax.random.fold_in(_rk, 2), 18), (1024,), 10, 12498, jnp.int32), jax.random.randint(jax.random.fold_in(jax.random.fold_in(_rk, 2), 19), (1024,), 0, 99999, jnp.int32), jax.random.randint(jax.random.fold_in(jax.random.fold_in(_rk, 2), 20), (1024,), 0, 99995, jnp.int32), jax.random.randint(jax.random.fold_in(jax.random.fold_in(_rk, 2), 21), (1024,), 1, 99998, jnp.int32), jax.random.randint(jax.random.fold_in(jax.random.fold_in(_rk, 2), 22), (1024,), 1, 99997, jnp.int32), jax.random.randint(jax.random.fold_in(jax.random.fold_in(_rk, 2), 23), (1024,), 2, 99989, jnp.int32), jax.random.randint(jax.random.fold_in(jax.random.fold_in(_rk, 2), 24), (1024,), 6, 12500, jnp.int32), jax.random.randint(jax.random.fold_in(jax.random.fold_in(_rk, 2), 25), (1024,), 2, 99995, jnp.int32)], axis=1)
        return (r_numerical_input, r_categorical_inputs)
    r_numerical_input, r_categorical_inputs = _rec_inputs()

    def _L0_rec_setup():
        import jax, jax.numpy as jnp
        import numpy as np
        B = 2048
        NUM_DENSE = 13
        NUM_TABLES = 26
        VOCAB = 12500
        D = 128
        BOT = [512, 256, 128]
        TOP = [1024, 1024, 512, 256, 1]
        TOP_IN = 27 * 26 // 2 + D + 1

        def _linear_params(key, fan_in, fan_out):
            kw, kb = jax.random.split(key)
            w = jax.random.normal(kw, (fan_out, fan_in), jnp.float32) * np.sqrt(2.0 / (fan_in + fan_out))
            b = jax.random.normal(kb, (fan_out,), jnp.float32) * np.sqrt(1.0 / fan_out)
            return (w, b)

        def _dlrm_forward(numerical_input, categorical_inputs, emb_tables, bot_params, top_params):
            x = numerical_input
            for w, b in bot_params:
                x = jax.nn.relu(x @ w.T + b)
            bottom = x
            emb = jax.vmap(lambda tbl, idx: tbl[idx])(emb_tables, categorical_inputs.T)
            concat = jnp.concatenate([bottom[:, None, :], jnp.transpose(emb, (1, 0, 2))], axis=1)
            inter = jnp.einsum('bnd,bmd->bnm', concat, concat)
            ti, tj = jnp.tril_indices(NUM_TABLES + 1, -1)
            inter_flat = inter[:, ti, tj]
            pad = jnp.zeros((numerical_input.shape[0], 1), dtype=bottom.dtype)
            y = jnp.concatenate([bottom, inter_flat, pad], axis=1)
            for w, b in top_params[:-1]:
                y = jax.nn.relu(y @ w.T + b)
            w, b = top_params[-1]
            return y @ w.T + b
        key = jax.random.key(seed)
        ks = jax.random.split(key, 16)
        numerical_input = jax.random.normal(ks[0], (B, NUM_DENSE), jnp.float32)
        categorical_inputs = jax.random.randint(ks[1], (B, NUM_TABLES), 0, VOCAB, jnp.int64 if jax.config.jax_enable_x64 else jnp.int32)
        bound = np.sqrt(1.0 / VOCAB)
        emb_tables = jax.random.uniform(ks[2], (NUM_TABLES, VOCAB, D), jnp.float32, -bound, bound)
        bw0, bb0 = _linear_params(ks[3], NUM_DENSE, BOT[0])
        bw1, bb1 = _linear_params(ks[4], BOT[0], BOT[1])
        bw2, bb2 = _linear_params(ks[5], BOT[1], BOT[2])
        tw0, tb0 = _linear_params(ks[6], TOP_IN, TOP[0])
        tw0 = tw0.at[:, -1].set(0.0)
        tw1, tb1 = _linear_params(ks[7], TOP[0], TOP[1])
        tw2, tb2 = _linear_params(ks[8], TOP[1], TOP[2])
        tw3, tb3 = _linear_params(ks[9], TOP[2], TOP[3])
        tw4, tb4 = _linear_params(ks[10], TOP[3], TOP[4])
        return dict(numerical_input=numerical_input, categorical_inputs=categorical_inputs, emb_tables=emb_tables, bw0=bw0, bb0=bb0, bw1=bw1, bb1=bb1, bw2=bw2, bb2=bb2, tw0=tw0, tb0=tb0, tw1=tw1, tb1=tb1, tw2=tw2, tb2=tb2, tw3=tw3, tb3=tb3, tw4=tw4, tb4=tb4)
    _L0_rec_all = _L0_rec_setup()
    _L0_rec_in = {k: v for k, v in _L0_rec_all.items() if k in ('emb_tables', 'bw0', 'bb0', 'bw1', 'bb1', 'bw2', 'bb2', 'tw0', 'tb0', 'tw1', 'tb1', 'tw2', 'tb2', 'tw3', 'tb3', 'tw4', 'tb4')}
    del _L0_rec_all
    return {'r_numerical_input': r_numerical_input, 'r_categorical_inputs': r_categorical_inputs, 'L0_rec_emb_tables': _L0_rec_in['emb_tables'], 'L0_rec_bw0': _L0_rec_in['bw0'], 'L0_rec_bb0': _L0_rec_in['bb0'], 'L0_rec_bw1': _L0_rec_in['bw1'], 'L0_rec_bb1': _L0_rec_in['bb1'], 'L0_rec_bw2': _L0_rec_in['bw2'], 'L0_rec_bb2': _L0_rec_in['bb2'], 'L0_rec_tw0': _L0_rec_in['tw0'], 'L0_rec_tb0': _L0_rec_in['tb0'], 'L0_rec_tw1': _L0_rec_in['tw1'], 'L0_rec_tb1': _L0_rec_in['tb1'], 'L0_rec_tw2': _L0_rec_in['tw2'], 'L0_rec_tb2': _L0_rec_in['tb2'], 'L0_rec_tw3': _L0_rec_in['tw3'], 'L0_rec_tb3': _L0_rec_in['tb3'], 'L0_rec_tw4': _L0_rec_in['tw4'], 'L0_rec_tb4': _L0_rec_in['tb4']}

def reference(r_numerical_input, r_categorical_inputs, L0_rec_emb_tables, L0_rec_bw0, L0_rec_bb0, L0_rec_bw1, L0_rec_bb1, L0_rec_bw2, L0_rec_bb2, L0_rec_tw0, L0_rec_tb0, L0_rec_tw1, L0_rec_tb1, L0_rec_tw2, L0_rec_tb2, L0_rec_tw3, L0_rec_tb3, L0_rec_tw4, L0_rec_tb4):
    import jax
    import jax.numpy as jnp

    def _L0_rec_ref(numerical_input, categorical_inputs, emb_tables, bw0, bb0, bw1, bb1, bw2, bb2, tw0, tb0, tw1, tb1, tw2, tb2, tw3, tb3, tw4, tb4):
        import jax, jax.numpy as jnp
        import numpy as np
        B = 2048
        NUM_DENSE = 13
        NUM_TABLES = 26
        VOCAB = 12500
        D = 128
        BOT = [512, 256, 128]
        TOP = [1024, 1024, 512, 256, 1]
        TOP_IN = 27 * 26 // 2 + D + 1

        def _linear_params(key, fan_in, fan_out):
            kw, kb = jax.random.split(key)
            w = jax.random.normal(kw, (fan_out, fan_in), jnp.float32) * np.sqrt(2.0 / (fan_in + fan_out))
            b = jax.random.normal(kb, (fan_out,), jnp.float32) * np.sqrt(1.0 / fan_out)
            return (w, b)

        def _dlrm_forward(numerical_input, categorical_inputs, emb_tables, bot_params, top_params):
            x = numerical_input
            for w, b in bot_params:
                x = jax.nn.relu(x @ w.T + b)
            bottom = x
            emb = jax.vmap(lambda tbl, idx: tbl[idx])(emb_tables, categorical_inputs.T)
            concat = jnp.concatenate([bottom[:, None, :], jnp.transpose(emb, (1, 0, 2))], axis=1)
            inter = jnp.einsum('bnd,bmd->bnm', concat, concat)
            ti, tj = jnp.tril_indices(NUM_TABLES + 1, -1)
            inter_flat = inter[:, ti, tj]
            pad = jnp.zeros((numerical_input.shape[0], 1), dtype=bottom.dtype)
            y = jnp.concatenate([bottom, inter_flat, pad], axis=1)
            for w, b in top_params[:-1]:
                y = jax.nn.relu(y @ w.T + b)
            w, b = top_params[-1]
            return y @ w.T + b
        bot = [(bw0, bb0), (bw1, bb1), (bw2, bb2)]
        top = [(tw0, tb0), (tw1, tb1), (tw2, tb2), (tw3, tb3), (tw4, tb4)]
        return _dlrm_forward(numerical_input, categorical_inputs, emb_tables, bot, top)
    y = _L0_rec_ref(r_numerical_input, r_categorical_inputs, L0_rec_emb_tables, L0_rec_bw0, L0_rec_bb0, L0_rec_bw1, L0_rec_bb1, L0_rec_bw2, L0_rec_bb2, L0_rec_tw0, L0_rec_tb0, L0_rec_tw1, L0_rec_tb1, L0_rec_tw2, L0_rec_tb2, L0_rec_tw3, L0_rec_tb3, L0_rec_tw4, L0_rec_tb4)
    return y

_drawn_inputs = setup_inputs


def setup_inputs(seed=0):
    import zlib

    import numpy as np

    out = dict(_drawn_inputs(seed))
    spreads = {}
    factors = {}
    for name, (base, spread) in spreads.items():
        noise = np.random.default_rng([zlib.crc32(name.encode()), seed]).standard_normal(out[name].shape)
        drawn = base * np.exp(spread * noise) if base else spread * noise
        out[name] = jnp.asarray(drawn.astype(out[name].dtype))
    for name, factor in factors.items():
        out[name] = (out[name] * factor).astype(out[name].dtype)
    return out
```

```python
from contextlib import ExitStack

import concourse.bass as bass
import concourse.mybir as mybir

F32 = mybir.dt.float32
F32R = mybir.dt.float32r
I32 = mybir.dt.int32
ALU = mybir.AluOpType
ACT = mybir.ActivationFunctionType

P = 128
B = 1024
TILES = B // P
GROUP = 2
GROUPS = TILES // GROUP
N = GROUP * P
DENSE = 13
TABLES = 26
D = 128
BOT = (512, 256, 128)
TOP = (1024, 1024, 512, 256)
PAIRS = TABLES * (TABLES + 1) // 2
TOP_IN = D + PAIRS + 1

HALF = TABLES // 2
TURNS = (4, 3, 3, 3)
TURN0 = tuple(sum(TURNS[:q]) for q in range(4))
NT = 2 * len(TURNS)
SLOT = 32
QUAD = 4
QROWS = P // QUAD
SPANS = 4
SPAN = QROWS // SPANS
PER_BANK = 4
PAIR_DMAS = [(j, r) for j in range(1, TABLES + 1) for r in range(3)
             if max(j * (j - 1) // 2, r * P) < min(j * (j + 1) // 2, (r + 1) * P)]

KCH = (4, 8, 8, 4)
LAST_ROWS = TOP_IN - 3 * P
STAGE = 1024
STAGES = 3
W_OFF = [sum(KCH[m] * TOP[m] for m in range(n)) for n in range(4)]
W_COLS = W_OFF[3] + KCH[3] * TOP[3]
LOADS = W_COLS // STAGE

BOT_BLOCKS = [(n, m) for n in range(3) for m in range(BOT[n] // P)]
TOP_BLOCKS = [(n, m) for n in range(4) for m in range(TOP[n] // P)]
HID = len(TOP_BLOCKS) - TOP[3] // P
NB = len(TOP_BLOCKS) + 1
BOT_HALVES = 2
BOT_N = B // BOT_HALVES
BOT_NB = len(BOT_BLOCKS) * BOT_HALVES
PART0 = [0, 8, 16]

VECS = (4, 2, 1, 8, 8, 4, 2, 2)
V_BOT = (0, 4, 6)
V_TOP = (7, 15, 23, 27)
V_LAST = 29


def tile_units(d):
    return [("turn", d, c) for c in range(NT)] + [("dots", d, s) for s in range(SPANS)]


def group_order(lead, until):
    units = tile_units(0) + tile_units(1)
    cost = [KCH[n] for n, _ in TOP_BLOCKS]
    order = units[:lead] + [("split",)]
    rest = units[lead:]
    done = placed = 0
    for i, c in enumerate(cost):
        order.append(("block", i))
        done += c
        due = min(len(rest), int(len(rest) * done / (sum(cost) * until)))
        order += rest[placed:due]
        placed = due
    return order + [("last",)]


ORDER = group_order(4, 0.8)
END_ORDER = [("split",)] + [("block", i) for i in range(len(TOP_BLOCKS))] + [("last",)]


def start_order():
    bot = [("bottom", h, i) for h in range(BOT_HALVES) for i in range(len(BOT_BLOCKS))]
    units = tile_units(0) + tile_units(1)
    order, w = [], 0
    for n, b in enumerate(bot):
        order.append(b)
        if n >= 7:
            order.append(units.pop(0))
        if n >= 1:
            order.append(("weights", w))
            w += 1
    while units:
        order.append(units.pop(0))
        if w < LOADS:
            order.append(("weights", w))
            w += 1
    return order


START_ORDER = start_order()


def build(nc, xT, idx, tables, bw0, bw1, bw2, w0, w1, w2, w3, vecs, last_bias, out):
    with ExitStack() as ctx:
        def sb(name, shape, dt, stack=ctx):
            return stack.enter_context(nc.sbuf_tensor(name, shape, dt))

        def sem(name):
            return ctx.enter_context(nc.semaphore(name))

        w_hi = sb("w_hi", [P, W_COLS], F32R)
        w_lo = sb("w_lo", [P, W_COLS], F32R)
        bottom = sb("bottom", [P, B], F32)
        ident = sb("ident", [P, P], F32)
        vec = sb("vec", [P, sum(VECS)], F32)
        bias4 = sb("bias4", [P, 1], F32)
        rows_of = sb("rows_of", [P, TILES * TABLES], I32)
        rows_now = sb("rows_now", [P, 2, TABLES], I32)
        gathered = sb("gathered", [P, HALF, D], F32)
        vT = sb("vT", [P, QROWS, QUAD, SLOT], F32)
        pairs = sb("pairs", [P, 3, N], F32)
        relu = sb("relu", [P, 2, N], F32)
        y = sb("y", [P, TILES], F32)

        with ExitStack() as first:
            idx_raw = sb("idx_raw", [P, TILES * TABLES], I32, first)
            idx_wrap = sb("idx_wrap", [P, TILES * TABLES], I32, first)
            x_in = sb("x_in", [DENSE, B], F32, first)
            bw0_sb = sb("bw0_sb", [DENSE, BOT[0]], F32, first)
            bw1_sb = sb("bw1_sb", [P, BOT[0] // P, BOT[1]], F32, first)
            bw2_sb = sb("bw2_sb", [P, BOT[1] // P, BOT[2]], F32, first)
            hb0 = sb("hb0", [P, BOT[0] // P, BOT_N], F32, first)
            hb1 = sb("hb1", [P, BOT[1] // P, BOT_N], F32, first)
            stage = sb("stage", [P, STAGES, STAGE], F32, first)
        dots_j = sb("dots_j", [64, HALF, P], F32)
        h_a = sb("h_a", [P, 8, 2, N], F32R)
        h_b = sb("h_b", [P, 8, 2, N], F32R)

        acc = ctx.enter_context(nc.psum_tensor("acc", [P, 2, 512], F32))
        turned = ctx.enter_context(nc.psum_tensor("turned", [P, 2, 512], F32))
        dots = ctx.enter_context(nc.psum_tensor("dots", [P, 2, 2, 512], F32))

        small_in = sem("small_in")
        idx_in = sem("idx_in")
        stage_in = [sem(f"stage_in{s}") for s in range(STAGES)]
        w_hi_done = sem("w_hi_done")
        w_lo_done = sem("w_lo_done")
        ident_zero = sem("ident_zero")
        ident_done = sem("ident_done")
        base_done = sem("base_done")
        idx_steps = sem("idx_steps")
        rows_copied = sem("rows_copied")
        rows_in = [sem(f"rows_in{q}") for q in range(len(TURNS))]
        part_free = sem("part_free")
        turn_done = sem("turn_done")
        vT_act = sem("vT_act")
        vT_dve = sem("vT_dve")
        vT_pads = sem("vT_pads")
        vT_bottom = sem("vT_bottom")
        span_done = sem("span_done")
        span_act = sem("span_act")
        span_dve = sem("span_dve")
        pairs_zero = sem("pairs_zero")
        pairs_in = sem("pairs_in")
        x_hi_done = sem("x_hi_done")
        x_lo_done = sem("x_lo_done")
        block_done = sem("block_done")
        block_read = sem("block_read")
        part_done = sem("part_done")
        y_out = sem("y_out")

        def w_part(w, n, k, m):
            at = W_OFF[n] + k * TOP[n] + m * P
            return w[0:P if (n, k) != (0, 3) else LAST_ROWS, at:at + P]

        def layer_in(n):
            return (h_b, h_a, h_b, h_a)[n]

        def out_of(n):
            return (h_a, h_b, h_a)[n]

        block = ctx.enter_context(nc.Block())

        @block.sync
        def _(sp):
            sp.dma_start(idx_raw[:], idx).then_inc(idx_in, 16)
            sp.dma_start(x_in[:], xT).then_inc(small_in, 16)
            sp.dma_start(bw0_sb[:], bw0).then_inc(small_in, 16)
            sp.dma_start(vec[:], vecs).then_inc(small_in, 16)
            sp.dma_start(bw1_sb[:], bw1.rearrange("(k p) o -> p k o", p=P)).then_inc(small_in, 16)
            sp.dma_start(bw2_sb[:], bw2.rearrange("(k p) o -> p k o", p=P)).then_inc(small_in, 16)
            sp.dma_start(bias4[:], last_bias.to_broadcast([P, 1])).then_inc(small_in, 16)

            def load_weights(n):
                s = n % STAGES
                if n >= STAGES:
                    sp.wait_ge(w_lo_done, n - STAGES + 1)
                layer = max(m for m in range(4) if W_OFF[m] <= n * STAGE)
                src = (w0, w1, w2, w3)[layer]
                chunks = STAGE // TOP[layer]
                k = (n * STAGE - W_OFF[layer]) // TOP[layer]
                rows = LAST_ROWS if (layer, k) == (0, 3) else P
                sp.dma_start(stage[0:rows, s, :].rearrange("p (k o) -> p k o", k=chunks),
                             src[k * P:k * P + chunks * rows, :].rearrange("(k p) o -> p k o", p=rows)
                             ).then_inc(stage_in[s], 16)

            def move_pairs(t, d):
                sp.wait_ge(span_act, SPANS * (t + 1))
                sp.wait_ge(span_dve, SPANS * (t + 1))
                for j, r in PAIR_DMAS:
                    first_pair = max(j * (j - 1) // 2, r * P)
                    i = first_pair - j * (j - 1) // 2
                    n = min(j * (j + 1) // 2, (r + 1) * P) - first_pair
                    at = 32 * ((j - 1) // HALF) + i
                    sp.dma_start(pairs[first_pair - r * P:first_pair - r * P + n, r, d * P:(d + 1) * P],
                                 dots_j[at:at + n, (j - 1) % HALF, :]).then_inc(pairs_in, 16)

            for n in range(LOADS):
                load_weights(n)
            sp.wait_ge(pairs_zero, 1)
            for d in range(GROUP):
                move_pairs(d, d)
            with sp.Fori(1, GROUPS) as k:
                sp.wait_ge(x_lo_done, 2 * k)
                for d in range(GROUP):
                    move_pairs(GROUP * k + d, d)
            sp.wait_ge(block_read, BOT_NB + NB * GROUPS)
            sp.dma_start(out.rearrange("(p t) o -> p (t o)", p=P), y[:]).then_inc(y_out, 16)
            sp.wait_ge(y_out, 16)

        @block.gpsimd
        def _(pool):
            nc.gpsimd.iota(rows_of[:], [[0, TILES], [tables.shape[0] // TABLES, TABLES]],
                           base=0, channel_multiplier=0).then_inc(base_done, 1)
            nc.gpsimd.memset(ident[:], 0.0).then_inc(ident_zero, 1)
            pool.wait_ge(ident_zero, 1)
            nc.gpsimd.affine_select(out=ident[:], in_=ident[:], compare_op=ALU.not_equal, fill=1.0, base=0,
                                    pattern=[[-1, P]], channel_multiplier=1).then_inc(ident_done, 1)

            def take_rows(t, d):
                nc.gpsimd.tensor_copy(rows_now[:, d, :], rows_of[:, bass.ds(t * TABLES, TABLES)]
                                      ).then_inc(rows_copied, 1)

            def gather(t, d, half, first_use=False):
                for q, n in enumerate(TURNS):
                    if not first_use:
                        pool.wait_ge(turn_done, NT * t + 4 * half + q - 3)
                        pool.sem_inc(part_free, 1)
                    for e in range(TURN0[q], TURN0[q] + n):
                        c = HALF * half + e
                        nc.gpsimd.indirect_dma_start(
                            gathered[:, e, :], None, tables,
                            bass.IndirectOffsetOnAxis(ap=rows_now[:, d, c:c + 1], axis=0)
                        ).then_inc(rows_in[q], 16)

            pool.wait_ge(idx_steps, 4)
            take_rows(0, 0)
            take_rows(1, 1)
            pool.wait_ge(rows_copied, 2)
            gather(0, 0, 0, first_use=True)
            gather(0, 0, 1)
            for half in range(2):
                gather(1, 1, half)
            with pool.Fori(1, GROUPS) as k:
                for q, n in enumerate(TURNS):
                    pool.wait_ge(rows_in[q], 16 * n * 2 * GROUP * k)
                for d in range(GROUP):
                    take_rows(GROUP * k + d, d)
                pool.wait_ge(rows_copied, GROUP * (k + 1))
                for d in range(GROUP):
                    for half in range(2):
                        gather(GROUP * k + d, d, half)

        @block.tensor
        def _(pe):
            def products(out_ap, terms, done):
                for n, (lhsT, rhs) in enumerate(terms):
                    last = nc.tensor.matmul(out_ap, lhsT, rhs, start=(n == 0), stop=(n == len(terms) - 1))
                last.then_inc(done, 1)

            def bottom_block(h, i):
                n, m = BOT_BLOCKS[i]
                b = len(BOT_BLOCKS) * h + i
                if b >= 2:
                    pe.wait_ge(block_read, b - 1)
                if m == 0 and b > 0:
                    pe.wait_ge(block_read, b)
                o = slice(m * P, (m + 1) * P)
                if n == 0:
                    terms = [(bw0_sb[:, o], x_in[:, h * BOT_N:(h + 1) * BOT_N])]
                elif n == 1:
                    terms = [(bw1_sb[:, k, o], hb0[:, k, :]) for k in range(BOT[0] // P)]
                else:
                    terms = [(bw2_sb[:, k, o], hb1[:, k, :]) for k in range(BOT[1] // P)]
                products(acc[:, b % 2, 0:BOT_N], terms, block_done)

            def turn(t, c, first_use=False):
                q, half = c % 4, c // 4
                pe.wait_ge(rows_in[q], 16 * TURNS[q] * (2 * t + half + 1))
                if not first_use:
                    pe.wait_ge(vT_act if c % 2 else vT_dve, 4 * t + c // 2)
                for e in range(TURNS[q]):
                    last = nc.tensor.transpose(turned[:, c % 2, e * P:(e + 1) * P],
                                               gathered[:, TURN0[q] + e, :], ident[:])
                last.then_inc(turn_done, 1)

            def span(t, s, first_use=False):
                if s == 0:
                    pe.wait_ge(vT_act, 4 * (t + 1))
                    pe.wait_ge(vT_dve, 4 * (t + 1))
                    pe.wait_ge(vT_bottom, t + 1)
                if not first_use:
                    pe.wait_ge(span_act, SPANS * t + s - 1)
                    pe.wait_ge(span_dve, SPANS * t + s - 1)
                for e in range(SPAN):
                    a = SPAN * s + e
                    at = (e % PER_BANK) * QUAD * TABLES
                    last = nc.tensor.matmul(dots[:, s % 2, e // PER_BANK, at:at + QUAD * TABLES],
                                            vT[:, a].rearrange("p q n -> p (q n)"), vT[:, a, :, 1:TABLES + 1],
                                            start=True, stop=True)
                last.then_inc(span_done, 1)

            def top_block(g, i):
                n, m = TOP_BLOCKS[i]
                pe.wait_ge(block_read, BOT_NB + NB * g + i - 1)
                h = layer_in(n)
                for k in range(KCH[n]):
                    if m == 0 and n == 0 and k < 2:
                        pe.wait_ge(x_lo_done, 2 * g + k + 1)
                    if m == 0 and n > 0:
                        pe.wait_ge(part_done, HID * g + PART0[n - 1] + k + 1)
                    r = LAST_ROWS if (n, k) == (0, 3) else P
                    for f, (w, part) in enumerate(((w_hi, 0), (w_hi, 1), (w_lo, 0))):
                        last = nc.tensor.matmul(acc[:, i % 2, 0:N], w_part(w, n, k, m), h[0:r, k, part, :],
                                                start=(k == 0 and f == 0), stop=(k == KCH[n] - 1 and f == 2))
                last.then_inc(block_done, 1)

            def last_layer(g):
                pe.wait_ge(block_read, BOT_NB + NB * g + NB - 1)
                for d in range(GROUP):
                    for k in range(TOP[3] // P):
                        last = nc.tensor.matmul(acc[:, 1, d:d + 1], relu[:, k, d * P:(d + 1) * P],
                                                vec[:, V_LAST + k:V_LAST + k + 1],
                                                start=(k == 0), stop=(k == TOP[3] // P - 1))
                last.then_inc(block_done, 1)

            pe.wait_ge(small_in, 16 * 6)
            pe.wait_ge(ident_done, 1)
            pe.wait_ge(vT_pads, 1)
            for step in START_ORDER:
                if step[0] == "bottom":
                    bottom_block(*step[1:])
                if step[0] == "turn":
                    turn(step[1], step[2], first_use=(step[1] == 0 and step[2] < 2))
                if step[0] == "dots":
                    span(step[1], step[2], first_use=(step[1] == 0 and step[2] < 2))
            pe.wait_ge(w_lo_done, LOADS)
            with pe.Fori(0, GROUPS - 1) as g:
                for step in ORDER:
                    if step[0] == "turn":
                        turn(GROUP * (g + 1) + step[1], step[2])
                    if step[0] == "dots":
                        span(GROUP * (g + 1) + step[1], step[2])
                    if step[0] == "block":
                        top_block(g, step[1])
                    if step[0] == "last":
                        last_layer(g)
            for i in range(len(TOP_BLOCKS)):
                top_block(GROUPS - 1, i)
            last_layer(GROUPS - 1)

        def copy_turn(engine_copy, t, c):
            q, half = c % 4, c // 4
            first_slot = 1 + HALF * half + TURN0[q]
            return engine_copy(vT[:, :, :, first_slot:first_slot + TURNS[q]].rearrange("p a q n -> p n q a"),
                               turned[:, c % 2, 0:TURNS[q] * P].rearrange("p (n q a) -> p n q a", q=QUAD, a=QROWS))

        def copy_span(engine_copy, s, g, upper):
            rows = TABLES if upper else HALF
            b0 = g * QROWS + s * SPAN
            src = dots[32 * g:32 * g + rows, s % 2, :, 0:PER_BANK * QUAD * TABLES].rearrange(
                "p b (a q j) -> p b a q j", a=PER_BANK, q=QUAD)[:, :, :, g, HALF * upper:HALF * (upper + 1)]
            dst = dots_j[32 * upper:32 * upper + rows, :, b0:b0 + SPAN].rearrange(
                "p j (b a) -> p b a j", a=PER_BANK)
            return engine_copy(dst, src)

        SPAN_ACT = ((0, 0), (0, 1))
        SPAN_DVE = tuple((g, u) for g in range(1, QUAD) for u in range(2))

        @block.scalar
        def _(act):
            def bottom_block(h, i):
                n, m = BOT_BLOCKS[i]
                b = len(BOT_BLOCKS) * h + i
                act.wait_ge(block_done, b + 1)
                dst = bottom[:, h * BOT_N:(h + 1) * BOT_N] if n == 2 else (hb0, hb1)[n][:, m, :]
                nc.scalar.activation(dst, acc[:, b % 2, 0:BOT_N], ACT.Relu,
                                     bias=vec[:, V_BOT[n] + m:V_BOT[n] + m + 1]).then_inc(block_read, 1)

            def weights_high(n):
                act.wait_ge(stage_in[n % STAGES], 16 * (n // STAGES + 1))
                rows = LAST_ROWS if n == KCH[0] - 1 else P
                nc.scalar.copy(w_hi[0:rows, n * STAGE:(n + 1) * STAGE], stage[0:rows, n % STAGES, :]
                               ).then_inc(w_hi_done, 1)

            def turn(t, c):
                if c == 0:
                    act.wait_ge(turn_done, NT * t + 1)
                    nc.scalar.copy(vT[:, :, :, 0].rearrange("p a q -> p q a"),
                                   bottom[:, bass.ds(t * P, P)].rearrange("p (q a) -> p q a", q=QUAD)
                                   ).then_inc(vT_bottom, 1)
                if c % 2:
                    act.wait_ge(turn_done, NT * t + c + 1)
                    copy_turn(nc.scalar.copy, t, c).then_inc(vT_act, 1)

            def span(t, s, first_use=False):
                if s == 0 and not first_use:
                    act.wait_ge(pairs_in, 16 * len(PAIR_DMAS) * t)
                act.wait_ge(span_done, SPANS * t + s + 1)
                for g, upper in SPAN_ACT:
                    last = copy_span(nc.scalar.copy, s, g, upper)
                last.then_inc(span_act, 1)

            def split_input(g):
                nc.scalar.copy(h_b[:, 0, 0, :], bottom[:, bass.ds(g * N, N)]).then_inc(x_hi_done, 1)
                act.wait_ge(pairs_in, 16 * len(PAIR_DMAS) * GROUP * (g + 1))
                nc.scalar.copy(h_b[:, 1:4, 0, :], pairs[:]).then_inc(x_hi_done, 1)

            def top_block(g, i):
                n, m = TOP_BLOCKS[i]
                bias = vec[:, V_TOP[n] + m:V_TOP[n] + m + 1]
                act.wait_ge(block_done, BOT_NB + NB * g + i + 1)
                if i < HID:
                    if i >= 2:
                        act.wait_ge(part_done, HID * g + i - 1)
                    nc.scalar.activation(relu[:, i % 2, :], acc[:, i % 2, 0:N], ACT.Relu, bias=bias)
                    nc.scalar.activation(out_of(n)[:, m, 0, :], acc[:, i % 2, 0:N], ACT.Relu, bias=bias
                                         ).then_inc(block_read, 1)
                else:
                    act.wait_ge(part_done, HID * g + min(i - 1, HID))
                    nc.scalar.activation(relu[:, i % 2, :], acc[:, i % 2, 0:N], ACT.Relu, bias=bias
                                         ).then_inc(block_read, 1)

            def last_layer(g):
                act.wait_ge(block_done, BOT_NB + NB * (g + 1))
                nc.scalar.activation(y[:, bass.ds(g * GROUP, GROUP)], acc[:, 1, 0:GROUP], ACT.Identity,
                                     bias=bias4[:, 0:1]).then_inc(block_read, 1)

            act.wait_ge(small_in, 16 * 6)
            for step in START_ORDER:
                if step[0] == "bottom":
                    bottom_block(*step[1:])
                if step[0] == "weights":
                    weights_high(step[1])
                if step[0] == "turn":
                    if step[1:] == (0, 0):
                        act.wait_ge(block_read, len(BOT_BLOCKS))
                    turn(*step[1:])
                if step[0] == "dots":
                    if step[1:] == (0, 0):
                        act.wait_ge(block_done, BOT_NB)
                    span(step[1], step[2], first_use=(step[1] == 0))
            act.wait_ge(block_read, BOT_NB)
            act.wait_ge(w_lo_done, LOADS)
            with act.Fori(0, GROUPS - 1) as g:
                for step in ORDER:
                    if step[0] == "turn":
                        turn(GROUP * (g + 1) + step[1], step[2])
                    if step[0] == "dots":
                        span(GROUP * (g + 1) + step[1], step[2])
                    if step[0] == "split":
                        split_input(g)
                    if step[0] == "block":
                        top_block(g, step[1])
                    if step[0] == "last":
                        last_layer(g)
            split_input(GROUPS - 1)
            for i in range(len(TOP_BLOCKS)):
                top_block(GROUPS - 1, i)
            last_layer(GROUPS - 1)

        @block.vector
        def _(dve):
            def low_part(out_ap, whole, high, done):
                nc.vector.tensor_tensor(out_ap, whole, high.bitcast(F32), ALU.subtract).then_inc(done, 1)

            def weights_low(n):
                rows = LAST_ROWS if n == KCH[0] - 1 else P
                cols = slice(n * STAGE, (n + 1) * STAGE)
                dve.wait_ge(w_hi_done, n + 1)
                low_part(w_lo[0:rows, cols], stage[0:rows, n % STAGES, :], w_hi[0:rows, cols], w_lo_done)

            def turn(t, c):
                if c % 2 == 0:
                    dve.wait_ge(turn_done, NT * t + c + 1)
                    copy_turn(nc.vector.tensor_copy, t, c).then_inc(vT_dve, 1)

            def span(t, s, first_use=False):
                if s == 0 and not first_use:
                    dve.wait_ge(pairs_in, 16 * len(PAIR_DMAS) * t)
                dve.wait_ge(span_done, SPANS * t + s + 1)
                for g, upper in SPAN_DVE:
                    last = copy_span(nc.vector.tensor_copy, s, g, upper)
                last.then_inc(span_dve, 1)

            def split_input(g):
                dve.wait_ge(x_hi_done, 2 * g + 1)
                low_part(h_b[:, 0, 1, :], bottom[:, bass.ds(g * N, N)], h_b[:, 0, 0, :], x_lo_done)
                dve.wait_ge(x_hi_done, 2 * g + 2)
                low_part(h_b[:, 1:4, 1, :], pairs[:], h_b[:, 1:4, 0, :], x_lo_done)

            def top_block(g, i):
                if i < HID:
                    n, m = TOP_BLOCKS[i]
                    h = out_of(n)
                    dve.wait_ge(block_read, BOT_NB + NB * g + i + 1)
                    low_part(h[:, m, 1, :], relu[:, i % 2, :], h[:, m, 0, :], part_done)

            vocab = tables.shape[0] // TABLES
            dve.wait_ge(idx_in, 16)
            nc.vector.tensor_scalar(idx_wrap[:], idx_raw[:], 0, vocab, ALU.is_lt, ALU.mult).then_inc(idx_steps, 1)
            dve.wait_ge(idx_steps, 1)
            nc.vector.tensor_tensor(idx_wrap[:], idx_raw[:], idx_wrap[:], ALU.add).then_inc(idx_steps, 1)
            dve.wait_ge(idx_steps, 2)
            nc.vector.tensor_scalar(idx_raw[:], idx_wrap[:], 0, vocab - 1, ALU.max, ALU.min).then_inc(idx_steps, 1)
            dve.wait_ge(idx_steps, 3)
            dve.wait_ge(base_done, 1)
            nc.vector.tensor_tensor(rows_of[:], rows_of[:], idx_raw[:], ALU.add).then_inc(idx_steps, 1)
            nc.vector.memset(vT[:, :, :, TABLES + 1:SLOT], 0.0).then_inc(vT_pads, 1)
            nc.vector.memset(pairs[:, 2, :], 0.0).then_inc(pairs_zero, 1)
            for step in START_ORDER:
                if step[0] == "weights":
                    weights_low(step[1])
                if step[0] == "turn":
                    turn(*step[1:])
                if step[0] == "dots":
                    span(step[1], step[2], first_use=(step[1] == 0))
            with dve.Fori(0, GROUPS - 1) as g:
                for step in ORDER:
                    if step[0] == "turn":
                        turn(GROUP * (g + 1) + step[1], step[2])
                    if step[0] == "dots":
                        span(GROUP * (g + 1) + step[1], step[2])
                    if step[0] == "split":
                        split_input(g)
                    if step[0] == "block":
                        top_block(g, step[1])
            split_input(GROUPS - 1)
            for i in range(HID):
                top_block(GROUPS - 1, i)


def kernel(**inputs):
    import numpy as np
    import concourse.bacc as bacc
    from concourse.bass_utils import run_bass_kernel_spmd as run

    a = {k.removeprefix("L0_rec_"): np.asarray(v) for k, v in inputs.items()}

    def by_block(v):
        return v.reshape(-1, P).T

    xT = a["r_numerical_input"].reshape(P, TILES, DENSE).transpose(2, 1, 0).reshape(DENSE, B)
    idx = a["r_categorical_inputs"].reshape(P, TILES * TABLES)
    vecs = np.concatenate([by_block(a[k]) for k in ("bb0", "bb1", "bb2", "tb0", "tb1", "tb2", "tb3")]
                          + [by_block(a["tw4"].reshape(-1))], axis=1)
    arrays = {
        "xT": xT, "idx": idx, "tables": a["emb_tables"].reshape(-1, D),
        "bw0": a["bw0"].T, "bw1": a["bw1"].T, "bw2": a["bw2"].T,
        "w0": a["tw0"].T, "w1": a["tw1"].T, "w2": a["tw2"].T, "w3": a["tw3"].T,
        "vecs": vecs, "last_bias": a["tb4"].reshape(1, 1),
    }
    arrays = {k: np.ascontiguousarray(v) for k, v in arrays.items()}
    nc = bacc.Bacc("TRN2", target_bir_lowering=False, num_devices=1)
    args = [nc.dram_tensor(k, v.shape, mybir.dt.from_np(v.dtype), kind="ExternalInput").ap()
            for k, v in arrays.items()]
    out = nc.dram_tensor("out", (B, 1), F32, kind="ExternalOutput").ap()
    build(nc, *args, out)
    return run(nc, [arrays], core_ids=[0]).results[0]["out"]
```

```python
from contextlib import ExitStack

import concourse.bass as bass
import concourse.mybir as mybir

F32 = mybir.dt.float32
F32R = mybir.dt.float32r
I32 = mybir.dt.int32
ALU = mybir.AluOpType
ACT = mybir.ActivationFunctionType

P = 128
B = 1024
TILES = B // P
GROUPS = TILES // 2
N = 2 * P
DENSE = 13
TABLES = 26
D = 128
BOT = (512, 256, 128)
TOP = (1024, 1024, 512, 256)
PAIRS = TABLES * (TABLES + 1) // 2
TOP_IN = D + PAIRS + 1

HALF = TABLES // 2
TURNS = (4, 3, 3, 3)
TURN0 = tuple(sum(TURNS[:q]) for q in range(4))
NT = 2 * len(TURNS)
SLOT = 32
QUAD = 4
QROWS = P // QUAD
SPANS = 4
SPAN = QROWS // SPANS
PER_BANK = 4

SMALL = 14
SMALL_HALF = SMALL // 2


def big_column(c, r):
    return 18 - r + 4 * c


def small_place():
    place = []
    for c in range(3):
        for r in range(4):
            j, at = 11 + r - 4 * c, 32 * r + big_column(c, r)
            place.append((j, c, at))
            if c == 2 and r < 2:
                place.append((2 - r, c, at + j))
    return place


SMALL_PLACE = small_place()

KCH = (4, 8, 8, 4)
STAGE = 1024
STAGES = 3
W_OFF = [sum(KCH[m] * TOP[m] for m in range(n)) for n in range(4)]
W_COLS = W_OFF[3] + KCH[3] * TOP[3]
LOADS = W_COLS // STAGE

BOT_BLOCKS = [(n, m) for n in range(3) for m in range(BOT[n] // P)]
TOP_BLOCKS = [(n, m) for n in range(4) for m in range(TOP[n] // P)]
HID = len(TOP_BLOCKS) - TOP[3] // P
NB = len(TOP_BLOCKS) + 1
BOT_HALVES = 2
BOT_N = B // BOT_HALVES
BOT_NB = len(BOT_BLOCKS) * BOT_HALVES
PART0 = [0, 8, 16]

VECS = (4, 2, 1, 8, 8, 4, 2, 2)
V_BOT = (0, 4, 6)
V_TOP = (7, 15, 23, 27)
V_LAST = 29


def tile_units(d):
    return [("turn", d, c) for c in range(NT)] + [("dots", d, s) for s in range(SPANS)]


LEAD = 4
UNTIL = 0.65


def group_order(next_units, lead_units):
    cost = [KCH[n] for n, _ in TOP_BLOCKS]
    order = []
    done = 0
    placed = [0, 0]
    for i, c in enumerate(cost):
        order.append(("block", i))
        done += c / sum(cost)
        for n, (units, share) in enumerate(((next_units, done / UNTIL),
                                            (lead_units, (done - UNTIL) / (1 - UNTIL)))):
            due = max(0, min(len(units), int(len(units) * share + 1e-6)))
            order += units[placed[n]:due]
            placed[n] = max(due, placed[n])
        if i == HID - 1:
            order.append(("split",))
    return order + [("last",)]


PAIR_UNITS = tile_units(0) + tile_units(1)
ORDER = group_order(PAIR_UNITS[LEAD:], [("turn", 2, c) for c in range(LEAD)])
NEXT_LAST_ORDER = group_order(PAIR_UNITS[LEAD:], [])
LAST_ORDER = [("block", i) for i in range(len(TOP_BLOCKS))] + [("last",)]


def start_order():
    bot = [("bottom", h, i) for h in range(BOT_HALVES) for i in range(len(BOT_BLOCKS))]
    units = tile_units(0) + tile_units(1) + [("turn", 2, c) for c in range(LEAD)]
    order, w = [], 0
    for n, b in enumerate(bot):
        order.append(b)
        if n in (3, 4, 5, 6, 8, 10, 11, 12, 13):
            order.append(units.pop(0))
        order.append(("weights", w))
        w += 1
    while units or w < LOADS:
        if units:
            order.append(units.pop(0))
        if w < LOADS:
            order.append(("weights", w))
            w += 1
    return order + [("split",)]


START_ORDER = start_order()


def build(nc, xT, idx, tables, bw0, bw1, bw2, w0, w1, w2, w3, vecs, last_bias, out):
    with ExitStack() as ctx:
        def sb(name, shape, dt, stack=ctx):
            return stack.enter_context(nc.sbuf_tensor(name, shape, dt))

        def sem(name):
            return ctx.enter_context(nc.semaphore(name))

        w_hi = sb("w_hi", [P, W_COLS], F32R)
        w_lo = sb("w_lo", [P, W_COLS], F32R)
        bottom = sb("bottom", [P, B], F32)
        ident = sb("ident", [P, P], F32)
        vec = sb("vec", [P, sum(VECS)], F32)
        bias4 = sb("bias4", [P, 1], F32)
        rows_of = sb("rows_of", [P, TILES * TABLES], I32)
        rows_now = sb("rows_now", [P, 2, TABLES], I32)
        gathered = sb("gathered", [P, HALF, D], F32)
        vT = sb("vT", [P, QROWS, QUAD, SLOT], F32)
        pairs = sb("pairs", [P, 3, 2, P], F32)
        relu = sb("relu", [P, 2, N], F32)
        y = sb("y", [P, TILES], F32)

        with ExitStack() as first:
            idx_raw = sb("idx_raw", [P, TILES * TABLES], I32, first)
            idx_wrap = sb("idx_wrap", [P, TILES * TABLES], I32, first)
            x_in = sb("x_in", [DENSE, B], F32, first)
            bw0_sb = sb("bw0_sb", [DENSE, BOT[0]], F32, first)
            bw1_sb = sb("bw1_sb", [P, BOT[0] // P, BOT[1]], F32, first)
            bw2_sb = sb("bw2_sb", [P, BOT[1] // P, BOT[2]], F32, first)
            hb0 = sb("hb0", [P, BOT[0] // P, BOT_N], F32, first)
            hb1 = sb("hb1", [P, BOT[1] // P, BOT_N], F32, first)
            stage = sb("stage", [P, STAGES, STAGE], F32, first)
        dots_j = sb("dots_j", [32 + SMALL_HALF, SMALL_HALF, P], F32)
        h_a = sb("h_a", [P, 8, 2, N], F32R)
        h_b = sb("h_b", [P, 8, 2, N], F32R)

        acc = ctx.enter_context(nc.psum_tensor("acc", [P, 2, 512], F32))
        turned = ctx.enter_context(nc.psum_tensor("turned", [P, 2, 512], F32))
        dots = ctx.enter_context(nc.psum_tensor("dots", [P, 2, 2, 512], F32))

        small_in = sem("small_in")
        idx_in = sem("idx_in")
        stage_in = [sem(f"stage_in{s}") for s in range(STAGES)]
        w_hi_done = sem("w_hi_done")
        w_lo_done = sem("w_lo_done")
        ident_zero = sem("ident_zero")
        ident_done = sem("ident_done")
        base_done = sem("base_done")
        idx_steps = sem("idx_steps")
        rows_copied = sem("rows_copied")
        rows_in = [sem(f"rows_in{q}") for q in range(len(TURNS))]
        part_free = sem("part_free")
        turn_done = sem("turn_done")
        vT_act = sem("vT_act")
        vT_dve = sem("vT_dve")
        vT_pads = sem("vT_pads")
        vT_bottom = sem("vT_bottom")
        span_done = sem("span_done")
        span_act = sem("span_act")
        span_dve = sem("span_dve")
        pairs_zero = sem("pairs_zero")
        pairs_in = sem("pairs_in")
        x_hi_done = sem("x_hi_done")
        x_lo_done = sem("x_lo_done")
        block_done = sem("block_done")
        block_read = sem("block_read")
        part_done = sem("part_done")
        y_out = sem("y_out")

        def w_part(w, n, k, m):
            at = W_OFF[n] + k * TOP[n] + m * P
            return w[:, at:at + P]

        def rows_of_group(g):
            return bass.ds(g * N, N)

        def layer_in(n):
            return (h_b, h_a, h_b, h_a)[n]

        def out_of(n):
            return (h_a, h_b, h_a)[n]

        block = ctx.enter_context(nc.Block())

        @block.sync
        def _(sp):
            sp.dma_start(idx_raw[:], idx).then_inc(idx_in, 16)
            sp.dma_start(x_in[:], xT).then_inc(small_in, 16)
            sp.dma_start(bw0_sb[:], bw0).then_inc(small_in, 16)
            sp.dma_start(vec[:], vecs).then_inc(small_in, 16)
            sp.dma_start(bw1_sb[:], bw1.rearrange("(k p) o -> p k o", p=P)).then_inc(small_in, 16)
            sp.dma_start(bw2_sb[:], bw2.rearrange("(k p) o -> p k o", p=P)).then_inc(small_in, 16)
            sp.dma_start(bias4[:], last_bias.to_broadcast([P, 1])).then_inc(small_in, 16)

            def load_weights(n):
                s = n % STAGES
                if n >= STAGES:
                    sp.wait_ge(w_lo_done, n - STAGES + 1)
                layer = max(m for m in range(4) if W_OFF[m] <= n * STAGE)
                src = (w0, w1, w2, w3)[layer]
                chunks = STAGE // TOP[layer]
                k = (n * STAGE - W_OFF[layer]) // TOP[layer]
                sp.dma_start(stage[:, s, :].rearrange("p (k o) -> p k o", k=chunks),
                             src[k * P:(k + chunks) * P, :].rearrange("(k p) o -> p k o", p=P)
                             ).then_inc(stage_in[s], 16)

            def move_pairs(t, d):
                sp.wait_ge(span_act, SPANS * (t + 1))
                sp.wait_ge(span_dve, SPANS * (t + 1))
                for j, c, at in SMALL_PLACE:
                    lower = j <= SMALL_HALF
                    sp.dma_start(pairs[at:at + j, c, d, :],
                                 dots_j[32 * lower:32 * lower + j, (j - 1) % SMALL_HALF, :]
                                 ).then_inc(pairs_in, 16)

            for n in range(LOADS):
                load_weights(n)
            with sp.Fori(0, GROUPS) as g:
                for d in range(2):
                    move_pairs(2 * g + d, d)
            sp.wait_ge(block_read, BOT_NB + NB * GROUPS)
            sp.dma_start(out.rearrange("(p t) o -> p (t o)", p=P), y[:]).then_inc(y_out, 16)
            sp.wait_ge(y_out, 16)

        @block.gpsimd
        def _(pool):
            nc.gpsimd.iota(rows_of[:], [[0, TILES], [tables.shape[0] // TABLES, TABLES]],
                           base=0, channel_multiplier=0).then_inc(base_done, 1)
            nc.gpsimd.memset(ident[:], 0.0).then_inc(ident_zero, 1)
            pool.wait_ge(ident_zero, 1)
            nc.gpsimd.affine_select(out=ident[:], in_=ident[:], compare_op=ALU.not_equal, fill=1.0, base=0,
                                    pattern=[[-1, P]], channel_multiplier=1).then_inc(ident_done, 1)

            def take_rows(t, d):
                nc.gpsimd.tensor_copy(rows_now[:, d, :], rows_of[:, bass.ds(t * TABLES, TABLES)]
                                      ).then_inc(rows_copied, 1)

            def gather(t, d, half, first_use=False):
                for q, n in enumerate(TURNS):
                    if not first_use:
                        pool.wait_ge(turn_done, NT * t + 4 * half + q - 3)
                        pool.sem_inc(part_free, 1)
                    for e in range(TURN0[q], TURN0[q] + n):
                        c = HALF * half + e
                        nc.gpsimd.indirect_dma_start(
                            gathered[:, e, :], None, tables,
                            bass.IndirectOffsetOnAxis(ap=rows_now[:, d, c:c + 1], axis=0)
                        ).then_inc(rows_in[q], 16)

            pool.wait_ge(idx_steps, 4)
            take_rows(0, 0)
            take_rows(1, 1)
            pool.wait_ge(rows_copied, 2)
            gather(0, 0, 0, first_use=True)
            gather(0, 0, 1)
            for half in range(2):
                gather(1, 1, half)
            with pool.Fori(1, TILES // 2) as k:
                for q, n in enumerate(TURNS):
                    pool.wait_ge(rows_in[q], 16 * n * 2 * 2 * k)
                for d in range(2):
                    take_rows(2 * k + d, d)
                pool.wait_ge(rows_copied, 2 * (k + 1))
                for d in range(2):
                    for half in range(2):
                        gather(2 * k + d, d, half)

        @block.tensor
        def _(pe):
            def products(out_ap, terms, done):
                for n, (lhsT, rhs) in enumerate(terms):
                    last = nc.tensor.matmul(out_ap, lhsT, rhs, start=(n == 0), stop=(n == len(terms) - 1))
                last.then_inc(done, 1)

            def bottom_block(h, i):
                n, m = BOT_BLOCKS[i]
                b = len(BOT_BLOCKS) * h + i
                if b >= 2:
                    pe.wait_ge(block_read, b - 1)
                if m == 0 and b > 0:
                    pe.wait_ge(block_read, b)
                o = slice(m * P, (m + 1) * P)
                if n == 0:
                    terms = [(bw0_sb[:, o], x_in[:, h * BOT_N:(h + 1) * BOT_N])]
                elif n == 1:
                    terms = [(bw1_sb[:, k, o], hb0[:, k, :]) for k in range(BOT[0] // P)]
                else:
                    terms = [(bw2_sb[:, k, o], hb1[:, k, :]) for k in range(BOT[1] // P)]
                products(acc[:, b % 2, 0:BOT_N], terms, block_done)

            def turn(t, c, first_use=False):
                q, half = c % 4, c // 4
                pe.wait_ge(rows_in[q], 16 * TURNS[q] * (2 * t + half + 1))
                if not first_use:
                    pe.wait_ge(vT_act if c % 2 else vT_dve, 4 * t + c // 2)
                for e in range(TURNS[q]):
                    last = nc.tensor.transpose(turned[:, c % 2, e * P:(e + 1) * P],
                                               gathered[:, TURN0[q] + e, :], ident[:])
                last.then_inc(turn_done, 1)

            def span(t, s, first_use=False):
                if s == 0:
                    pe.wait_ge(vT_act, 4 * (t + 1))
                    pe.wait_ge(vT_dve, 4 * (t + 1))
                    pe.wait_ge(vT_bottom, t + 1)
                if not first_use:
                    pe.wait_ge(span_act, SPANS * t + s - 1)
                    pe.wait_ge(span_dve, SPANS * t + s - 1)
                for e in range(SPAN):
                    a = SPAN * s + e
                    at = (e % PER_BANK) * QUAD * TABLES
                    last = nc.tensor.matmul(dots[:, s % 2, e // PER_BANK, at:at + QUAD * TABLES],
                                            vT[:, a].rearrange("p q n -> p (q n)"), vT[:, a, :, 1:TABLES + 1],
                                            start=True, stop=True)
                last.then_inc(span_done, 1)

            def top_block(g, i):
                n, m = TOP_BLOCKS[i]
                pe.wait_ge(block_read, BOT_NB + NB * g + i - 1)
                h = layer_in(n)
                for k in range(KCH[n]):
                    if m == 0 and n == 0 and k < 2:
                        pe.wait_ge(x_lo_done, 2 * g + k + 1)
                    if m == 0 and n > 0:
                        pe.wait_ge(part_done, HID * g + PART0[n - 1] + k + 1)
                    for f, (w, part) in enumerate(((w_hi, 0), (w_hi, 1), (w_lo, 0))):
                        last = nc.tensor.matmul(acc[:, i % 2, 0:N], w_part(w, n, k, m), h[:, k, part, 0:N],
                                                start=(k == 0 and f == 0), stop=(k == KCH[n] - 1 and f == 2))
                last.then_inc(block_done, 1)

            def last_layer(g):
                pe.wait_ge(block_read, BOT_NB + NB * g + NB - 1)
                for d in range(2):
                    for k in range(TOP[3] // P):
                        last = nc.tensor.matmul(acc[:, 1, d:d + 1], relu[:, k, d * P:(d + 1) * P],
                                                vec[:, V_LAST + k:V_LAST + k + 1],
                                                start=(k == 0), stop=(k == TOP[3] // P - 1))
                last.then_inc(block_done, 1)

            pe.wait_ge(small_in, 16 * 6)
            pe.wait_ge(ident_done, 1)
            pe.wait_ge(vT_pads, 1)
            for step in START_ORDER:
                if step[0] == "bottom":
                    bottom_block(*step[1:])
                if step[0] == "turn":
                    turn(step[1], step[2], first_use=(step[1] == 0 and step[2] < 2))
                if step[0] == "dots":
                    span(step[1], step[2], first_use=(step[1] == 0 and step[2] < 2))
            pe.wait_ge(w_lo_done, LOADS)

            def run_group(order, g, t):
                for step in order:
                    if step[0] == "turn":
                        turn(t + step[1], step[2])
                    if step[0] == "dots":
                        span(t + step[1], step[2])
                    if step[0] == "block":
                        top_block(g, step[1])
                    if step[0] == "last":
                        last_layer(g)

            with pe.Fori(0, GROUPS - 2) as g:
                run_group(ORDER, g, 2 * g + 2)
            run_group(NEXT_LAST_ORDER, GROUPS - 2, TILES - 2)
            run_group(LAST_ORDER, GROUPS - 1, TILES)

        def copy_turn(engine_copy, t, c):
            q, half = c % 4, c // 4
            first_slot = 1 + HALF * half + TURN0[q]
            return engine_copy(vT[:, :, :, first_slot:first_slot + TURNS[q]].rearrange("p a q n -> p n q a"),
                               turned[:, c % 2, 0:TURNS[q] * P].rearrange("p (n q a) -> p n q a", q=QUAD, a=QROWS))

        def dots_of(g, rows, s, columns):
            return dots[32 * g:32 * g + rows, s % 2, :, 0:PER_BANK * QUAD * TABLES].rearrange(
                "p b (a q j) -> p b a q j", a=PER_BANK, q=QUAD)[:, :, :, g, columns]

        def copy_big(engine_copy, s, g, r, d):
            rows = big_column(2, r)
            b0 = g * QROWS + s * SPAN
            dst = pairs[32 * r:32 * r + rows, :, d, b0:b0 + SPAN].rearrange("p c (b a) -> p b a c", a=PER_BANK)
            return engine_copy(dst, dots_of(g, rows, s, slice(big_column(0, r) - 1, rows, 4)))

        def copy_small(engine_copy, s, g, lower):
            rows = SMALL_HALF if lower else SMALL
            b0 = g * QROWS + s * SPAN
            first = 0 if lower else SMALL_HALF
            dst = dots_j[32 * lower:32 * lower + rows, :, b0:b0 + SPAN].rearrange("p j (b a) -> p b a j", a=PER_BANK)
            return engine_copy(dst, dots_of(g, rows, s, slice(first, first + SMALL_HALF)))

        SPAN_ACT = (0,)
        SPAN_DVE = (1, 2, 3)

        def copy_span(engine_copy, s, quadrants, d):
            for g in quadrants:
                for lower in (True, False):
                    copy_small(engine_copy, s, g, lower)
                for r in range(4):
                    last = copy_big(engine_copy, s, g, r, d)
            return last

        @block.scalar
        def _(act):
            def bottom_block(h, i):
                n, m = BOT_BLOCKS[i]
                b = len(BOT_BLOCKS) * h + i
                act.wait_ge(block_done, b + 1)
                dst = bottom[:, h * BOT_N:(h + 1) * BOT_N] if n == 2 else (hb0, hb1)[n][:, m, :]
                nc.scalar.activation(dst, acc[:, b % 2, 0:BOT_N], ACT.Relu,
                                     bias=vec[:, V_BOT[n] + m:V_BOT[n] + m + 1]).then_inc(block_read, 1)

            def weights_high(n):
                act.wait_ge(stage_in[n % STAGES], 16 * (n // STAGES + 1))
                nc.scalar.copy(w_hi[:, n * STAGE:(n + 1) * STAGE], stage[:, n % STAGES, :]
                               ).then_inc(w_hi_done, 1)

            def turn(t, c):
                if c == NT - 1:
                    act.wait_ge(turn_done, NT * t + c + 1)
                    nc.scalar.copy(vT[:, :, :, 0].rearrange("p a q -> p q a"),
                                   bottom[:, bass.ds(t * P, P)].rearrange("p (q a) -> p q a", q=QUAD)
                                   ).then_inc(vT_bottom, 1)
                if c % 2:
                    act.wait_ge(turn_done, NT * t + c + 1)
                    copy_turn(nc.scalar.copy, t, c).then_inc(vT_act, 1)

            def span(t, s, d, first_use=False):
                if s == 0 and not first_use:
                    act.wait_ge(pairs_in, 16 * SMALL * t)
                    if not isinstance(t, int):
                        act.wait_ge(x_lo_done, t - d)
                act.wait_ge(span_done, SPANS * t + s + 1)
                copy_span(nc.scalar.copy, s, SPAN_ACT, d).then_inc(span_act, 1)

            def split_input(g):
                nc.scalar.copy(h_b[:, 0, 0, 0:N], bottom[:, rows_of_group(g)]).then_inc(x_hi_done, 1)
                act.wait_ge(pairs_in, 16 * SMALL * 2 * (g + 1))
                act.wait_ge(span_dve, SPANS * 2 * (g + 1))
                nc.scalar.copy(h_b[:, 1:4, 0, 0:N], pairs[:].rearrange("p c d b -> p c (d b)")).then_inc(x_hi_done, 1)

            def top_block(g, i):
                n, m = TOP_BLOCKS[i]
                bias = vec[:, V_TOP[n] + m:V_TOP[n] + m + 1]
                act.wait_ge(block_done, BOT_NB + NB * g + i + 1)
                if i < HID:
                    if i >= 2:
                        act.wait_ge(part_done, HID * g + i - 1)
                    nc.scalar.activation(relu[:, i % 2, 0:N], acc[:, i % 2, 0:N], ACT.Relu, bias=bias)
                    nc.scalar.activation(out_of(n)[:, m, 0, 0:N], acc[:, i % 2, 0:N], ACT.Relu, bias=bias
                                         ).then_inc(block_read, 1)
                else:
                    act.wait_ge(part_done, HID * g + min(i - 1, HID))
                    nc.scalar.activation(relu[:, i % 2, 0:N], acc[:, i % 2, 0:N], ACT.Relu, bias=bias
                                         ).then_inc(block_read, 1)

            def last_layer(g):
                act.wait_ge(block_done, BOT_NB + NB * (g + 1))
                nc.scalar.activation(y[:, bass.ds(2 * g, 2)], acc[:, 1, 0:2], ACT.Identity,
                                     bias=bias4[:, 0:1]).then_inc(block_read, 1)

            act.wait_ge(small_in, 16 * 6)
            for step in START_ORDER:
                if step[0] == "bottom":
                    bottom_block(*step[1:])
                if step[0] == "weights":
                    weights_high(step[1])
                if step[0] == "turn":
                    if step[1:] == (0, NT - 1):
                        act.wait_ge(block_read, len(BOT_BLOCKS))
                    turn(*step[1:])
                if step[0] == "dots":
                    if step[1:] == (0, 0):
                        act.wait_ge(block_done, BOT_NB)
                        act.wait_ge(pairs_zero, 1)
                    span(step[1], step[2], step[1], first_use=(step[1] == 0))
                if step[0] == "split":
                    act.wait_ge(block_read, BOT_NB)
                    act.wait_ge(w_lo_done, LOADS)
                    split_input(0)

            def run_group(order, g, t):
                for step in order:
                    if step[0] == "turn":
                        turn(t + step[1], step[2])
                    if step[0] == "dots":
                        span(t + step[1], step[2], step[1])
                    if step[0] == "split":
                        split_input(g + 1)
                    if step[0] == "block":
                        top_block(g, step[1])
                    if step[0] == "last":
                        last_layer(g)

            with act.Fori(0, GROUPS - 2) as g:
                run_group(ORDER, g, 2 * g + 2)
            run_group(NEXT_LAST_ORDER, GROUPS - 2, TILES - 2)
            run_group(LAST_ORDER, GROUPS - 1, TILES)

        @block.vector
        def _(dve):
            def low_part(out_ap, whole, high, done):
                nc.vector.tensor_tensor(out_ap, whole, high.bitcast(F32), ALU.subtract).then_inc(done, 1)

            def weights_low(n):
                cols = slice(n * STAGE, (n + 1) * STAGE)
                dve.wait_ge(w_hi_done, n + 1)
                low_part(w_lo[:, cols], stage[:, n % STAGES, :], w_hi[:, cols], w_lo_done)

            def turn(t, c):
                if c % 2 == 0:
                    dve.wait_ge(turn_done, NT * t + c + 1)
                    copy_turn(nc.vector.tensor_copy, t, c).then_inc(vT_dve, 1)

            def span(t, s, d, first_use=False):
                if s == 0 and not first_use:
                    dve.wait_ge(pairs_in, 16 * SMALL * t)
                    if not isinstance(t, int):
                        dve.wait_ge(x_lo_done, t - d)
                dve.wait_ge(span_done, SPANS * t + s + 1)
                copy_span(nc.vector.tensor_copy, s, SPAN_DVE, d).then_inc(span_dve, 1)

            def split_input(g):
                dve.wait_ge(x_hi_done, 2 * g + 1)
                low_part(h_b[:, 0, 1, 0:N], bottom[:, rows_of_group(g)], h_b[:, 0, 0, 0:N], x_lo_done)
                dve.wait_ge(x_hi_done, 2 * g + 2)
                low_part(h_b[:, 1:4, 1, 0:N], pairs[:].rearrange("p c d b -> p c (d b)"), h_b[:, 1:4, 0, 0:N], x_lo_done)

            def top_block(g, i):
                if i < HID:
                    n, m = TOP_BLOCKS[i]
                    h = out_of(n)
                    dve.wait_ge(block_read, BOT_NB + NB * g + i + 1)
                    low_part(h[:, m, 1, 0:N], relu[:, i % 2, 0:N], h[:, m, 0, 0:N], part_done)

            vocab = tables.shape[0] // TABLES
            dve.wait_ge(idx_in, 16)
            nc.vector.tensor_scalar(idx_wrap[:], idx_raw[:], 0, vocab, ALU.is_lt, ALU.mult).then_inc(idx_steps, 1)
            dve.wait_ge(idx_steps, 1)
            nc.vector.tensor_tensor(idx_wrap[:], idx_raw[:], idx_wrap[:], ALU.add).then_inc(idx_steps, 1)
            dve.wait_ge(idx_steps, 2)
            nc.vector.tensor_scalar(idx_raw[:], idx_wrap[:], 0, vocab - 1, ALU.max, ALU.min).then_inc(idx_steps, 1)
            dve.wait_ge(idx_steps, 3)
            dve.wait_ge(base_done, 1)
            nc.vector.tensor_tensor(rows_of[:], rows_of[:], idx_raw[:], ALU.add).then_inc(idx_steps, 1)
            nc.vector.memset(vT[:, :, :, TABLES + 1:SLOT], 0.0).then_inc(vT_pads, 1)
            nc.vector.memset(pairs[:], 0.0).then_inc(pairs_zero, 1)
            for step in START_ORDER:
                if step[0] == "weights":
                    weights_low(step[1])
                if step[0] == "turn":
                    turn(*step[1:])
                if step[0] == "dots":
                    if step[1:] == (0, 0):
                        dve.wait_ge(pairs_zero, 1)
                    span(step[1], step[2], step[1], first_use=(step[1] == 0))
                if step[0] == "split":
                    split_input(0)

            def run_group(order, g, t):
                for step in order:
                    if step[0] == "turn":
                        turn(t + step[1], step[2])
                    if step[0] == "dots":
                        span(t + step[1], step[2], step[1])
                    if step[0] == "split":
                        split_input(g + 1)
                    if step[0] == "block":
                        top_block(g, step[1])

            with dve.Fori(0, GROUPS - 2) as g:
                run_group(ORDER, g, 2 * g + 2)
            run_group(NEXT_LAST_ORDER, GROUPS - 2, TILES - 2)
            run_group(LAST_ORDER, GROUPS - 1, TILES)


def kernel(**inputs):
    import numpy as np
    import concourse.bacc as bacc
    from concourse.bass_utils import run_bass_kernel_spmd as run

    a = {k.removeprefix("L0_rec_"): np.asarray(v) for k, v in inputs.items()}

    def by_block(v):
        return v.reshape(-1, P).T

    xT = a["r_numerical_input"].reshape(P, TILES, DENSE).transpose(2, 1, 0).reshape(DENSE, B)
    idx = a["r_categorical_inputs"].reshape(P, TILES * TABLES)
    vecs = np.concatenate([by_block(a[k]) for k in ("bb0", "bb1", "bb2", "tb0", "tb1", "tb2", "tb3")]
                          + [by_block(a["tw4"].reshape(-1))], axis=1)
    pair = np.full((3, P), -1)
    for c in range(3):
        for r in range(4):
            j = big_column(c, r)
            pair[c, 32 * r:32 * r + j] = D + j * (j - 1) // 2 + np.arange(j)
    for j, c, at in SMALL_PLACE:
        pair[c, at:at + j] = D + j * (j - 1) // 2 + np.arange(j)
    pair[np.unravel_index(np.argmin(pair), pair.shape)] = TOP_IN - 1
    feature = np.concatenate([np.arange(D), pair.reshape(-1)])
    w0 = np.zeros((feature.size, TOP[0]), a["tw0"].dtype)
    w0[feature >= 0] = a["tw0"].T[feature[feature >= 0]]
    arrays = {
        "xT": xT, "idx": idx, "tables": a["emb_tables"].reshape(-1, D),
        "bw0": a["bw0"].T, "bw1": a["bw1"].T, "bw2": a["bw2"].T,
        "w0": w0, "w1": a["tw1"].T, "w2": a["tw2"].T, "w3": a["tw3"].T,
        "vecs": vecs, "last_bias": a["tb4"].reshape(1, 1),
    }
    arrays = {k: np.ascontiguousarray(v) for k, v in arrays.items()}
    nc = bacc.Bacc("TRN2", target_bir_lowering=False, num_devices=1)
    args = [nc.dram_tensor(k, v.shape, mybir.dt.from_np(v.dtype), kind="ExternalInput").ap()
            for k, v in arrays.items()]
    out = nc.dram_tensor("out", (B, 1), F32, kind="ExternalOutput").ap()
    build(nc, *args, out)
    return run(nc, [arrays], core_ids=[0]).results[0]["out"]
```

```python
from contextlib import ExitStack

import concourse.bass as bass
import concourse.mybir as mybir

F32 = mybir.dt.float32
F32R = mybir.dt.float32r
I32 = mybir.dt.int32
ALU = mybir.AluOpType
ACT = mybir.ActivationFunctionType

P = 128
B = 1024
TILES = B // P
GROUPS = TILES // 2
N = 2 * P
DENSE = 13
TABLES = 26
D = 128
BOT = (512, 256, 128)
TOP = (1024, 1024, 512, 256)
PAIRS = TABLES * (TABLES + 1) // 2
TOP_IN = D + PAIRS + 1

HALF = TABLES // 2
TURNS = (4, 3, 3, 3)
TURN0 = tuple(sum(TURNS[:q]) for q in range(4))
NT = 2 * len(TURNS)
SLOT = 32
QUAD = 4
QROWS = P // QUAD
SPANS = 4
SPAN = QROWS // SPANS
PER_BANK = 4

SMALL = 14
SMALL_HALF = SMALL // 2


def big_column(c, r):
    return 18 - r + 4 * c


def small_place():
    place = []
    for c in range(3):
        for r in range(4):
            j, at = 11 + r - 4 * c, 32 * r + big_column(c, r)
            place.append((j, c, at))
            if c == 2 and r < 2:
                place.append((2 - r, c, at + j))
    return place


SMALL_PLACE = small_place()

KCH = (4, 8, 8, 4)
STAGE = 1024
STAGES = 3
W_OFF = [sum(KCH[m] * TOP[m] for m in range(n)) for n in range(4)]
W_COLS = W_OFF[3] + KCH[3] * TOP[3]
LOADS = W_COLS // STAGE
LOADS_FIRST = 11

BOT_BLOCKS = [(n, m) for n in range(3) for m in range(BOT[n] // P)]
TOP_BLOCKS = [(n, m) for n in range(4) for m in range(TOP[n] // P)]
HID = len(TOP_BLOCKS) - TOP[3] // P
NB = len(TOP_BLOCKS) + 1
BOT_PARTS = GROUPS
BOT_N = B // BOT_PARTS
BOT_NB = len(BOT_BLOCKS) * BOT_PARTS


def bottom_order():
    first = [[(h, 0, m) for m in range(BOT[0] // P)] for h in range(BOT_PARTS)] + [[]]
    order = first[0]
    for h in range(BOT_PARTS):
        order = order + [(h, 1, 0)] + first[h + 1][:2] + [(h, 1, 1)] + first[h + 1][2:] + [(h, 2, 0)]
    return order


BOT_ORDER = bottom_order()


def bottom_read(h, n, m):
    return BOT_ORDER.index((h, n, m)) + 1


PART0 = [0, 8, 16]

SOLOS = 2
WIDE = [min(512, o) for o in TOP]
WIDE_BLOCKS = [(n, m) for n in range(4) for m in range(TOP[n] // WIDE[n])]
NW = len(WIDE_BLOCKS)
WIDE0 = [sum(TOP[m] // WIDE[m] for m in range(n)) for n in range(4)]
NS = WIDE0[3]


def blocks_before(g):
    return BOT_NB + NB * (g - 1)


def parts_before(g):
    return HID * (g - 1)


def inputs_before(g):
    return 2 * SOLOS + 2 * (g - 1)

VECS = (4, 2, 1, 8, 8, 4, 2, 2)
V_BOT = (0, 4, 6)
V_TOP = (7, 15, 23, 27)
V_LAST = 29


def tile_units(d):
    return [("turn", d, c) for c in range(NT)] + [("dots", d, s) for s in range(SPANS)]


LEAD = 7
PACE = 28


def group_order(units):
    order = []
    units = list(units)
    now = due = 0
    for i, (n, _) in enumerate(TOP_BLOCKS):
        order.append(("block", i))
        now += 3 * KCH[n]
        if i == HID - 1:
            order.append(("split",))
        while units and now >= due:
            unit = units.pop(0)
            order.append(unit)
            if unit[0] == "turn":
                now += TURNS[unit[2] % 4]
                due += PACE
                if unit[2] == NT - 1:
                    due = now + 1
            else:
                now += 2 * SPAN
                due = now + 1 if unit[2] == 1 else now
    return order + units + [("last",)]


PAIR_UNITS = tile_units(0) + tile_units(1)
ORDER = group_order(PAIR_UNITS[LEAD:] + [("turn", 2, c) for c in range(LEAD)])
NEXT_LAST_ORDER = group_order(PAIR_UNITS[LEAD:])
LAST_ORDER = [("block", i) for i in range(len(TOP_BLOCKS))] + [("last",)]


def solo_order():
    steps = []
    for t in range(SOLOS):
        for n in range(4):
            wides = [i for i, (layer, _) in enumerate(WIDE_BLOCKS) if layer == n]
            steps += [("wide", t, i) for i in wides] + [("flip", t, i) for i in wides]
        steps.append(("solo_last", t))
    for t in range(1, SOLOS):
        steps.remove(("wide", t, 0))
        steps.insert(steps.index(("wide", t - 1, NW - 1)), ("wide", t, 0))
    return steps


SOLO_ORDER = solo_order()
WIDE_ORDER = [step[1:] for step in SOLO_ORDER if step[0] == "wide"]


def wide_count(t, i):
    return WIDE_ORDER.index((t, i)) + 1


START_PLAN = """
    bbbbbTw bbTw bbTw bbbTw bbTw bbTw bbbTw bbTw  DDDDTT
    w bbbT w bbT w bbTTxW T WT FF  wDwDW w DTTD
    wWTF FTTwT W TTxF DD w W DTTDW F L
    WT FFTT W TTT DDW FDF TTD W TFTTTW FTLg
"""


def start_order():
    turns = [("turn", *divmod(n, NT)) for n in range(4 * NT + LEAD)]
    dots = [("dots", *divmod(n, SPANS)) for n in range(4 * SPANS)]
    solo = list(SOLO_ORDER)
    queues = {"b": [("bottom", *which) for which in BOT_ORDER], "w": [("weights", n) for n in range(LOADS)],
              "g": [("split",)], "T": turns, "D": dots, "x": [("solo_split", t) for t in range(SOLOS)],
              "W": solo, "F": solo, "L": solo}
    kinds = {"T": "turn", "D": "dots", "x": "solo_split", "W": "wide", "F": "flip", "L": "solo_last"}
    order = []
    for letter in "".join(START_PLAN.split()):
        order.append(queues[letter].pop(0))
        assert order[-1][0] == kinds.get(letter, order[-1][0]), order[-3:]
    assert not any(queues.values())
    return order


START_ORDER = start_order()


def build(nc, xT, idx, tables, bw0, bw1, bw2, w0, w1, w2, w3, vecs, last_bias, out):
    with ExitStack() as ctx:
        def sb(name, shape, dt, stack=ctx):
            return stack.enter_context(nc.sbuf_tensor(name, shape, dt))

        def sem(name):
            return ctx.enter_context(nc.semaphore(name))

        w_hi = sb("w_hi", [P, W_COLS], F32R)
        w_lo = sb("w_lo", [P, W_COLS], F32R)
        bottom = sb("bottom", [P, B], F32)
        ident = sb("ident", [P, P], F32)
        vec = sb("vec", [P, sum(VECS)], F32)
        bias4 = sb("bias4", [P, 1], F32)
        rows_of = sb("rows_of", [P, TILES * TABLES], I32)
        rows_now = sb("rows_now", [P, 2, TABLES], I32)
        gathered = sb("gathered", [P, HALF, D], F32)
        vT = sb("vT", [P, QROWS, QUAD, SLOT], F32)
        pairs = sb("pairs", [P, 3, 2, P], F32)
        with ExitStack() as before_relu:
            idx_raw = sb("idx_raw", [P, TILES * TABLES], I32, before_relu)
            idx_wrap = sb("idx_wrap", [P, TILES * TABLES], I32, before_relu)
        relu = sb("relu", [P, 2, N], F32)
        y = sb("y", [P, TILES], F32)

        dots_j = sb("dots_j", [32 + SMALL_HALF, SMALL_HALF, P], F32)

        with ExitStack() as first:
            hb0 = sb("hb0", [P, 2, BOT[0] // P, BOT_N], F32, first)
            sb("place_of_stage", [P, STAGES, STAGE], F32, first)
            x_in = sb("x_in", [DENSE, B], F32, first)
            bw0_sb = sb("bw0_sb", [DENSE, BOT[0]], F32, first)
            bw1_sb = sb("bw1_sb", [P, BOT[0] // P, BOT[1]], F32, first)
            bw2_sb = sb("bw2_sb", [P, BOT[1] // P, BOT[2]], F32, first)
            hb1 = sb("hb1", [P, BOT[1] // P, BOT_N], F32, first)
        with ExitStack() as second:
            s_a = sb("s_a", [P, 8, 2, P], F32R, second)
            stage = sb("stage", [P, STAGES, STAGE], F32, second)
            s_b = sb("s_b", [P, 8, 2, P], F32R, second)
            wide = sb("wide", [P, 2, 512], F32, second)
        h_a = sb("h_a", [P, 8, 2, N], F32R)
        h_b = sb("h_b", [P, 8, 2, N], F32R)

        acc = ctx.enter_context(nc.psum_tensor("acc", [P, 2, 512], F32))
        turned = ctx.enter_context(nc.psum_tensor("turned", [P, 2, 512], F32))
        dots = ctx.enter_context(nc.psum_tensor("dots", [P, 2, 2, 512], F32))

        small_in = sem("small_in")
        idx_in = sem("idx_in")
        stage_in = [sem(f"stage_in{s}") for s in range(STAGES)]
        w_hi_done = sem("w_hi_done")
        w_lo_done = sem("w_lo_done")
        ident_zero = sem("ident_zero")
        ident_done = sem("ident_done")
        base_done = sem("base_done")
        idx_steps = sem("idx_steps")
        rows_copied = sem("rows_copied")
        rows_in = [sem(f"rows_in{q}") for q in range(len(TURNS))]
        part_free = sem("part_free")
        turn_done = sem("turn_done")
        vT_act = sem("vT_act")
        vT_dve = sem("vT_dve")
        vT_pads = sem("vT_pads")
        vT_bottom = sem("vT_bottom")
        span_done = sem("span_done")
        span_act = sem("span_act")
        span_dve = sem("span_dve")
        pairs_zero = sem("pairs_zero")
        pairs_in = sem("pairs_in")
        x_hi_done = sem("x_hi_done")
        x_lo_done = sem("x_lo_done")
        block_done = sem("block_done")
        block_read = sem("block_read")
        part_done = sem("part_done")
        wide_done = sem("wide_done")
        wide_copied = sem("wide_copied")
        flip_done = sem("flip_done")
        flip_relu_act = sem("flip_relu_act")
        flip_relu_dve = sem("flip_relu_dve")
        flip_hi_act = sem("flip_hi_act")
        flip_hi_dve = sem("flip_hi_dve")
        flip_lo = sem("flip_lo")
        solo_done = sem("solo_done")
        solo_y = sem("solo_y")
        y_out = sem("y_out")

        def w_part(w, n, k, m):
            at = W_OFF[n] + k * TOP[n] + m * P
            return w[:, at:at + P]

        def rows_of_group(g):
            return bass.ds(g * N, N)

        def layer_in(n):
            return (h_b, h_a, h_b, h_a)[n]

        def out_of(n):
            return (h_a, h_b, h_a)[n]

        def solo_in(n):
            return (s_b, s_a, s_b, s_a)[n]

        def solo_out(n):
            return (s_a, s_b, s_a)[n]

        def relu_made(t, i):
            return (flip_relu_act if i % 2 else flip_relu_dve), NW // 2 * t + i // 2 + 1

        def wide_chunks(n, m, i):
            chunks = WIDE[n] // P
            return wide[:, i % 2, 0:WIDE[n]].rearrange("p (c b) -> p c b", b=P), m * chunks, chunks

        block = ctx.enter_context(nc.Block())

        @block.sync
        def _(sp):
            sp.dma_start(idx_raw[:], idx).then_inc(idx_in, 16)
            sp.dma_start(x_in[:], xT).then_inc(small_in, 16)
            sp.dma_start(bw0_sb[:], bw0).then_inc(small_in, 16)
            sp.dma_start(vec[:], vecs).then_inc(small_in, 16)
            sp.dma_start(bw1_sb[:], bw1.rearrange("(k p) o -> p k o", p=P)).then_inc(small_in, 16)
            sp.dma_start(bw2_sb[:], bw2.rearrange("(k p) o -> p k o", p=P)).then_inc(small_in, 16)
            sp.dma_start(bias4[:], last_bias.to_broadcast([P, 1])).then_inc(small_in, 16)

            def load_weights(n):
                s = n % STAGES
                if n >= STAGES:
                    sp.wait_ge(w_lo_done, n - STAGES + 1)
                layer = max(m for m in range(4) if W_OFF[m] <= n * STAGE)
                src = (w0, w1, w2, w3)[layer]
                chunks = STAGE // TOP[layer]
                k = (n * STAGE - W_OFF[layer]) // TOP[layer]
                sp.dma_start(stage[:, s, :].rearrange("p (k o) -> p k o", k=chunks),
                             src[k * P:(k + chunks) * P, :].rearrange("(k p) o -> p k o", p=P)
                             ).then_inc(stage_in[s], 16)

            def move_pairs(t, d):
                sp.wait_ge(span_act, SPANS * (t + 1))
                sp.wait_ge(span_dve, SPANS * (t + 1))
                for j, c, at in SMALL_PLACE:
                    lower = j <= SMALL_HALF
                    sp.dma_start(pairs[at:at + j, c, d, :],
                                 dots_j[32 * lower:32 * lower + j, (j - 1) % SMALL_HALF, :]
                                 ).then_inc(pairs_in, 16)

            for n in range(LOADS_FIRST):
                load_weights(n)
            move_pairs(0, 0)
            for n in range(LOADS_FIRST, LOADS):
                load_weights(n)
            move_pairs(1, 1)
            with sp.Fori(1, GROUPS) as g:
                for d in range(2):
                    move_pairs(2 * g + d, d)
            sp.wait_ge(block_read, blocks_before(GROUPS))
            sp.dma_start(out.rearrange("(p t) o -> p (t o)", p=P), y[:]).then_inc(y_out, 16)
            sp.wait_ge(y_out, 16)

        @block.gpsimd
        def _(pool):
            nc.gpsimd.iota(rows_of[:], [[0, TILES], [tables.shape[0] // TABLES, TABLES]],
                           base=0, channel_multiplier=0).then_inc(base_done, 1)
            nc.gpsimd.memset(ident[:], 0.0).then_inc(ident_zero, 1)
            pool.wait_ge(ident_zero, 1)
            nc.gpsimd.affine_select(out=ident[:], in_=ident[:], compare_op=ALU.not_equal, fill=1.0, base=0,
                                    pattern=[[-1, P]], channel_multiplier=1).then_inc(ident_done, 1)

            def take_rows(t, d):
                nc.gpsimd.tensor_copy(rows_now[:, d, :], rows_of[:, bass.ds(t * TABLES, TABLES)]
                                      ).then_inc(rows_copied, 1)

            def gather(t, d, half, first_use=False):
                for q, n in enumerate(TURNS):
                    if not first_use:
                        pool.wait_ge(turn_done, NT * t + 4 * half + q - 3)
                        pool.sem_inc(part_free, 1)
                    for e in range(TURN0[q], TURN0[q] + n):
                        c = HALF * half + e
                        nc.gpsimd.indirect_dma_start(
                            gathered[:, e, :], None, tables,
                            bass.IndirectOffsetOnAxis(ap=rows_now[:, d, c:c + 1], axis=0)
                        ).then_inc(rows_in[q], 16)

            pool.wait_ge(idx_steps, 4)
            take_rows(0, 0)
            take_rows(1, 1)
            pool.wait_ge(rows_copied, 2)
            gather(0, 0, 0, first_use=True)
            gather(0, 0, 1)
            for half in range(2):
                gather(1, 1, half)
            with pool.Fori(1, TILES // 2) as k:
                take_rows(2 * k, 0)
                pool.wait_ge(rows_copied, 2 * k + 1)
                gather(2 * k, 0, 0)
                take_rows(2 * k + 1, 1)
                pool.wait_ge(rows_copied, 2 * k + 2)
                gather(2 * k, 0, 1)
                for half in range(2):
                    gather(2 * k + 1, 1, half)

        @block.tensor
        def _(pe):
            def bottom_block(h, n, m):
                b = BOT_ORDER.index((h, n, m))
                if b >= 2:
                    pe.wait_ge(block_read, b - 1)
                o = slice(m * P, (m + 1) * P)
                if n == 0:
                    terms = [(bw0_sb[:, o], x_in[:, h * BOT_N:(h + 1) * BOT_N])]
                elif n == 1:
                    terms = [(bw1_sb[:, k, o], hb0[:, h % 2, k, :]) for k in range(BOT[0] // P)]
                else:
                    terms = [(bw2_sb[:, k, o], hb1[:, k, :]) for k in range(BOT[1] // P)]
                for k, (lhsT, rhs) in enumerate(terms):
                    if n > 0:
                        pe.wait_ge(block_read, bottom_read(h, n - 1, k))
                    last = nc.tensor.matmul(acc[:, b % 2, 0:BOT_N], lhsT, rhs,
                                            start=(k == 0), stop=(k == len(terms) - 1))
                last.then_inc(block_done, 1)

            def turn(t, c, first_use=False):
                q, half = c % 4, c // 4
                pe.wait_ge(rows_in[q], 16 * TURNS[q] * (2 * t + half + 1))
                if not first_use:
                    pe.wait_ge(vT_act if c % 2 else vT_dve, 4 * t + c // 2)
                for e in range(TURNS[q]):
                    last = nc.tensor.transpose(turned[:, c % 2, e * P:(e + 1) * P],
                                               gathered[:, TURN0[q] + e, :], ident[:])
                last.then_inc(turn_done, 1)

            def span(t, s, first_use=False):
                if s == 0:
                    pe.wait_ge(vT_act, 4 * (t + 1))
                    pe.wait_ge(vT_dve, 4 * (t + 1))
                    pe.wait_ge(vT_bottom, t + 1)
                if not first_use:
                    pe.wait_ge(span_act, SPANS * t + s - 1)
                    pe.wait_ge(span_dve, SPANS * t + s - 1)
                for e in range(SPAN):
                    a = SPAN * s + e
                    at = (e % PER_BANK) * QUAD * TABLES
                    last = nc.tensor.matmul(dots[:, s % 2, e // PER_BANK, at:at + QUAD * TABLES],
                                            vT[:, a].rearrange("p q n -> p (q n)"), vT[:, a, :, 1:TABLES + 1],
                                            start=True, stop=True)
                last.then_inc(span_done, 1)

            def top_block(g, i):
                n, m = TOP_BLOCKS[i]
                pe.wait_ge(block_read, blocks_before(g) + i - 1)
                h = layer_in(n)
                for k in range(KCH[n]):
                    if m == 0 and n == 0 and k < 2:
                        pe.wait_ge(x_lo_done, inputs_before(g) + k + 1)
                    if m == 0 and n > 0:
                        pe.wait_ge(part_done, parts_before(g) + PART0[n - 1] + k + 1)
                    for f, (w, part) in enumerate(((w_hi, 0), (w_hi, 1), (w_lo, 0))):
                        last = nc.tensor.matmul(acc[:, i % 2, 0:N], w_part(w, n, k, m), h[:, k, part, 0:N],
                                                start=(k == 0 and f == 0), stop=(k == KCH[n] - 1 and f == 2))
                last.then_inc(block_done, 1)

            def last_layer(g):
                pe.wait_ge(block_read, blocks_before(g + 1) - 1)
                for d in range(2):
                    for k in range(TOP[3] // P):
                        last = nc.tensor.matmul(acc[:, 1, d:d + 1], relu[:, k, d * P:(d + 1) * P],
                                                vec[:, V_LAST + k:V_LAST + k + 1],
                                                start=(k == 0), stop=(k == TOP[3] // P - 1))
                last.then_inc(block_done, 1)

            def wide_block(t, i):
                n, m = WIDE_BLOCKS[i]
                if i >= 2:
                    pe.wait_ge(*relu_made(t, i - 2))
                elif t == 0:
                    pe.wait_ge(block_read, BOT_NB)
                else:
                    pe.wait_ge(*relu_made(t - 1, NW - 2 + i))
                h = solo_in(n)
                for k in range(KCH[n]):
                    if t == 0 and m == 0:
                        pe.wait_ge(w_lo_done, (W_OFF[n] + k * TOP[n]) // STAGE + 1)
                    if m == 0 and n == 0 and k < 2:
                        pe.wait_ge(x_lo_done, 2 * t + k + 1)
                    if m == 0 and n > 0 and k % 4 == 0:
                        pe.wait_ge(flip_lo, NS * t + WIDE0[n - 1] + k // 4 + 1)
                    at = W_OFF[n] + k * TOP[n] + m * WIDE[n]
                    for f, (part, w) in enumerate(((0, w_hi), (0, w_lo), (1, w_hi))):
                        last = nc.tensor.matmul(acc[:, i % 2, 0:WIDE[n]], h[:, k, part, :], w[:, at:at + WIDE[n]],
                                                start=(k == 0 and f == 0), stop=(k == KCH[n] - 1 and f == 2))
                last.then_inc(wide_done, 1)

            def flip(t, i):
                pe.wait_ge(wide_copied, wide_count(t, i))
                if i == 0 and t > 0:
                    pe.wait_ge(solo_y, t)
                for c in range(WIDE[WIDE_BLOCKS[i][0]] // P):
                    last = nc.tensor.transpose(acc[:, i % 2, c * P:(c + 1) * P], wide[:, i % 2, c * P:(c + 1) * P],
                                               ident[:])
                last.then_inc(flip_done, 1)

            def solo_last(t):
                pe.wait_ge(*relu_made(t, NW - 1))
                if t < SOLOS - 1:
                    pe.wait_ge(wide_copied, wide_count(t + 1, 0))
                for k in range(TOP[3] // P):
                    last = nc.tensor.matmul(acc[:, 0, 0:1], wide[:, 1, k * P:(k + 1) * P],
                                            vec[:, V_LAST + k:V_LAST + k + 1],
                                            start=(k == 0), stop=(k == TOP[3] // P - 1))
                last.then_inc(solo_done, 1)

            pe.wait_ge(small_in, 16 * 6)
            pe.wait_ge(ident_done, 1)
            pe.wait_ge(vT_pads, 1)
            for step in START_ORDER:
                if step[0] == "bottom":
                    bottom_block(*step[1:])
                if step[0] == "turn":
                    turn(step[1], step[2], first_use=(step[1] == 0 and step[2] < 2))
                if step[0] == "dots":
                    span(step[1], step[2], first_use=(step[1] == 0 and step[2] < 2))
                if step[0] == "wide":
                    wide_block(*step[1:])
                if step[0] == "flip":
                    flip(*step[1:])
                if step[0] == "solo_last":
                    solo_last(step[1])

            def run_group(order, g, t):
                for step in order:
                    if step[0] == "turn":
                        turn(t + step[1], step[2])
                    if step[0] == "dots":
                        span(t + step[1], step[2])
                    if step[0] == "block":
                        top_block(g, step[1])
                    if step[0] == "last":
                        last_layer(g)

            with pe.Fori(1, GROUPS - 2) as g:
                run_group(ORDER, g, 2 * g + 2)
            run_group(NEXT_LAST_ORDER, GROUPS - 2, TILES - 2)
            run_group(LAST_ORDER, GROUPS - 1, TILES)

        def copy_turn(engine_copy, t, c):
            q, half = c % 4, c // 4
            first_slot = 1 + HALF * half + TURN0[q]
            return engine_copy(vT[:, :, :, first_slot:first_slot + TURNS[q]].rearrange("p a q n -> p n q a"),
                               turned[:, c % 2, 0:TURNS[q] * P].rearrange("p (n q a) -> p n q a", q=QUAD, a=QROWS))

        def dots_of(g, rows, s, columns):
            return dots[32 * g:32 * g + rows, s % 2, :, 0:PER_BANK * QUAD * TABLES].rearrange(
                "p b (a q j) -> p b a q j", a=PER_BANK, q=QUAD)[:, :, :, g, columns]

        def copy_big(engine_copy, s, g, r, d):
            rows = big_column(2, r)
            b0 = g * QROWS + s * SPAN
            dst = pairs[32 * r:32 * r + rows, :, d, b0:b0 + SPAN].rearrange("p c (b a) -> p b a c", a=PER_BANK)
            return engine_copy(dst, dots_of(g, rows, s, slice(big_column(0, r) - 1, rows, 4)))

        def copy_small(engine_copy, s, g, lower):
            rows = SMALL_HALF if lower else SMALL
            b0 = g * QROWS + s * SPAN
            first = 0 if lower else SMALL_HALF
            dst = dots_j[32 * lower:32 * lower + rows, :, b0:b0 + SPAN].rearrange("p j (b a) -> p b a j", a=PER_BANK)
            return engine_copy(dst, dots_of(g, rows, s, slice(first, first + SMALL_HALF)))

        SPAN_ACT = (0, 1)
        SPAN_DVE = (2, 3)

        def copy_span(engine_copy, s, quadrants, d):
            for g in quadrants:
                for lower in (True, False):
                    copy_small(engine_copy, s, g, lower)
                for r in range(4):
                    last = copy_big(engine_copy, s, g, r, d)
            return last

        @block.scalar
        def _(act):
            def bottom_block(h, n, m):
                b = BOT_ORDER.index((h, n, m))
                act.wait_ge(block_done, b + 1)
                if n == 0:
                    dst = hb0[:, h % 2, m, :]
                elif n == 1:
                    dst = hb1[:, m, :]
                else:
                    dst = bottom[:, h * BOT_N:(h + 1) * BOT_N]
                nc.scalar.activation(dst, acc[:, b % 2, 0:BOT_N], ACT.Relu,
                                     bias=vec[:, V_BOT[n] + m:V_BOT[n] + m + 1]).then_inc(block_read, 1)

            def weights_high(n):
                if n >= LOADS_FIRST:
                    act.wait_ge(stage_in[n % STAGES], 16 * (n // STAGES + 1))
                    nc.scalar.copy(w_hi[:, n * STAGE:(n + 1) * STAGE], stage[:, n % STAGES, :]
                                   ).then_inc(w_hi_done, 1)

            def turn(t, c):
                if c == NT - 1:
                    act.wait_ge(turn_done, NT * t + c + 1)
                    nc.scalar.copy(vT[:, :, :, 0].rearrange("p a q -> p q a"),
                                   bottom[:, bass.ds(t * P, P)].rearrange("p (q a) -> p q a", q=QUAD)
                                   ).then_inc(vT_bottom, 1)
                if c % 2:
                    if c < 2 and not (isinstance(t, int) and t == 0):
                        act.wait_ge(span_done, SPANS * t)
                    act.wait_ge(turn_done, NT * t + c + 1)
                    copy_turn(nc.scalar.copy, t, c).then_inc(vT_act, 1)

            def span(t, s, d, first_use=False):
                if s == 0 and not first_use:
                    act.wait_ge(pairs_in, 16 * SMALL * t)
                    if isinstance(t, int) and t < 4:
                        if t >= 2:
                            act.wait_ge(x_lo_done, 2 * (t - 1))
                    else:
                        act.wait_ge(x_lo_done, t - d + 2 * SOLOS - 2)
                act.wait_ge(span_done, SPANS * t + s + 1)
                copy_span(nc.scalar.copy, s, SPAN_ACT, d).then_inc(span_act, 1)

            def split_input(g):
                nc.scalar.copy(h_b[:, 0, 0, 0:N], bottom[:, rows_of_group(g)]).then_inc(x_hi_done, 1)
                act.wait_ge(pairs_in, 16 * SMALL * 2 * (g + 1))
                act.wait_ge(span_dve, SPANS * 2 * (g + 1))
                nc.scalar.copy(h_b[:, 1:4, 0, 0:N], pairs[:].rearrange("p c d b -> p c (d b)")).then_inc(x_hi_done, 1)

            def top_block(g, i):
                n, m = TOP_BLOCKS[i]
                bias = vec[:, V_TOP[n] + m:V_TOP[n] + m + 1]
                act.wait_ge(block_done, blocks_before(g) + i + 1)
                if i < HID:
                    if i >= 2:
                        act.wait_ge(part_done, parts_before(g) + i - 1)
                    nc.scalar.activation(relu[:, i % 2, 0:N], acc[:, i % 2, 0:N], ACT.Relu, bias=bias)
                    nc.scalar.activation(out_of(n)[:, m, 0, 0:N], acc[:, i % 2, 0:N], ACT.Relu, bias=bias
                                         ).then_inc(block_read, 1)
                else:
                    act.wait_ge(part_done, parts_before(g) + min(i - 1, HID))
                    nc.scalar.activation(relu[:, i % 2, 0:N], acc[:, i % 2, 0:N], ACT.Relu, bias=bias
                                         ).then_inc(block_read, 1)

            def last_layer(g):
                act.wait_ge(block_done, blocks_before(g + 1))
                nc.scalar.activation(y[:, bass.ds(2 * g, 2)], acc[:, 1, 0:2], ACT.Identity,
                                     bias=bias4[:, 0:1]).then_inc(block_read, 1)

            def solo_split(t):
                nc.scalar.copy(s_b[:, 0, 0, :], bottom[:, t * P:(t + 1) * P]).then_inc(x_hi_done, 1)
                act.wait_ge(pairs_in, 16 * SMALL * (t + 1))
                act.wait_ge(span_dve, SPANS * (t + 1))
                nc.scalar.copy(s_b[:, 1:4, 0, :], pairs[:, :, t, :]).then_inc(x_hi_done, 1)

            def wide_block(t, i):
                act.wait_ge(wide_done, wide_count(t, i))
                if i >= 2:
                    act.wait_ge(flip_lo, NS * t + i - 1)
                elif t > 0 and i == 0:
                    act.wait_ge(flip_lo, NS * t)
                elif t > 0:
                    act.wait_ge(solo_done, t)
                nc.scalar.copy(wide[:, i % 2, 0:WIDE[WIDE_BLOCKS[i][0]]],
                               acc[:, i % 2, 0:WIDE[WIDE_BLOCKS[i][0]]]).then_inc(wide_copied, 1)

            def flip(t, i):
                n, m = WIDE_BLOCKS[i]
                relus, k0, chunks = wide_chunks(n, m, i)
                if i % 2:
                    act.wait_ge(flip_done, NW * t + i + 1)
                    for c in range(chunks):
                        v = V_TOP[n] + k0 + c
                        last = nc.scalar.activation(relus[:, c, :], acc[:, 1, c * P:(c + 1) * P], ACT.Relu,
                                                    bias=vec[:, v:v + 1])
                    last.then_inc(flip_relu_act, 1)
                    if i < NS:
                        act.wait_ge(*relu_made(t, i))
                        nc.scalar.copy(solo_out(n)[:, k0:k0 + chunks, 0, :], relus).then_inc(flip_hi_act, 1)

            def solo_last(t):
                act.wait_ge(solo_done, t + 1)
                nc.scalar.activation(y[:, t:t + 1], acc[:, 0, 0:1], ACT.Identity,
                                     bias=bias4[:, 0:1]).then_inc(solo_y, 1)

            act.wait_ge(small_in, 16 * 6)
            for step in START_ORDER:
                if step[0] == "bottom":
                    bottom_block(*step[1:])
                if step[0] == "weights":
                    weights_high(step[1])
                if step[0] == "turn":
                    if step[2] == NT - 1:
                        act.wait_ge(block_read, bottom_read(step[1] * P // BOT_N, 2, 0))
                    turn(*step[1:])
                if step[0] == "dots":
                    if step[1:] == (0, 0):
                        act.wait_ge(pairs_zero, 1)
                    span(step[1], step[2], step[1] % 2, first_use=(step[1] == 0))
                if step[0] == "solo_split":
                    if step[1] == 0:
                        act.wait_ge(block_read, BOT_NB)
                    solo_split(step[1])
                if step[0] == "wide":
                    wide_block(*step[1:])
                if step[0] == "flip":
                    flip(*step[1:])
                if step[0] == "solo_last":
                    solo_last(step[1])
                if step[0] == "split":
                    act.wait_ge(w_lo_done, LOADS)
                    split_input(1)

            def run_group(order, g, t):
                for step in order:
                    if step[0] == "turn":
                        turn(t + step[1], step[2])
                    if step[0] == "dots":
                        span(t + step[1], step[2], step[1])
                    if step[0] == "split":
                        split_input(g + 1)
                    if step[0] == "block":
                        top_block(g, step[1])
                    if step[0] == "last":
                        last_layer(g)

            with act.Fori(1, GROUPS - 2) as g:
                run_group(ORDER, g, 2 * g + 2)
            run_group(NEXT_LAST_ORDER, GROUPS - 2, TILES - 2)
            run_group(LAST_ORDER, GROUPS - 1, TILES)

        @block.vector
        def _(dve):
            def low_part(out_ap, whole, high, done):
                nc.vector.tensor_tensor(out_ap, whole, high.bitcast(F32), ALU.subtract).then_inc(done, 1)

            def split_weights(n):
                cols = slice(n * STAGE, (n + 1) * STAGE)
                dve.wait_ge(stage_in[n % STAGES], 16 * (n // STAGES + 1))
                if n < LOADS_FIRST:
                    nc.vector.tensor_copy(w_hi[:, cols], stage[:, n % STAGES, :]).then_inc(w_hi_done, 1)
                dve.wait_ge(w_hi_done, n + 1)
                low_part(w_lo[:, cols], stage[:, n % STAGES, :], w_hi[:, cols], w_lo_done)

            def turn(t, c):
                if c % 2 == 0:
                    if c < 2 and not (isinstance(t, int) and t == 0):
                        dve.wait_ge(span_done, SPANS * t)
                    dve.wait_ge(turn_done, NT * t + c + 1)
                    copy_turn(nc.vector.tensor_copy, t, c).then_inc(vT_dve, 1)

            def span(t, s, d, first_use=False):
                if s == 0 and not first_use:
                    dve.wait_ge(pairs_in, 16 * SMALL * t)
                    if isinstance(t, int) and t < 4:
                        if t >= 2:
                            dve.wait_ge(x_lo_done, 2 * (t - 1))
                    else:
                        dve.wait_ge(x_lo_done, t - d + 2 * SOLOS - 2)
                dve.wait_ge(span_done, SPANS * t + s + 1)
                copy_span(nc.vector.tensor_copy, s, SPAN_DVE, d).then_inc(span_dve, 1)

            def split_input(g):
                dve.wait_ge(x_hi_done, inputs_before(g) + 1)
                low_part(h_b[:, 0, 1, 0:N], bottom[:, rows_of_group(g)], h_b[:, 0, 0, 0:N], x_lo_done)
                dve.wait_ge(x_hi_done, inputs_before(g) + 2)
                low_part(h_b[:, 1:4, 1, 0:N], pairs[:].rearrange("p c d b -> p c (d b)"), h_b[:, 1:4, 0, 0:N],
                         x_lo_done)

            def top_block(g, i):
                if i < HID:
                    n, m = TOP_BLOCKS[i]
                    h = out_of(n)
                    dve.wait_ge(block_read, blocks_before(g) + i + 1)
                    low_part(h[:, m, 1, 0:N], relu[:, i % 2, 0:N], h[:, m, 0, 0:N], part_done)

            def solo_split(t):
                dve.wait_ge(x_hi_done, 2 * t + 1)
                low_part(s_b[:, 0, 1, :], bottom[:, t * P:(t + 1) * P], s_b[:, 0, 0, :], x_lo_done)
                dve.wait_ge(x_hi_done, 2 * t + 2)
                low_part(s_b[:, 1:4, 1, :], pairs[:, :, t, :], s_b[:, 1:4, 0, :], x_lo_done)

            def flip(t, i):
                n, m = WIDE_BLOCKS[i]
                relus, k0, chunks = wide_chunks(n, m, i)
                if i % 2 == 0:
                    dve.wait_ge(flip_done, NW * t + i + 1)
                    for c in range(chunks):
                        v = V_TOP[n] + k0 + c
                        last = nc.vector.tensor_scalar(relus[:, c, :], acc[:, 0, c * P:(c + 1) * P],
                                                       vec[:, v:v + 1], 0.0, ALU.add, ALU.max)
                    last.then_inc(flip_relu_dve, 1)
                    dve.wait_ge(*relu_made(t, i))
                    nc.vector.tensor_copy(solo_out(n)[:, k0:k0 + chunks, 0, :], relus).then_inc(flip_hi_dve, 1)
                if i < NS:
                    made = flip_hi_act if i % 2 else flip_hi_dve
                    dve.wait_ge(made, (NS // 2 if i % 2 else NW // 2) * t + i // 2 + 1)
                    out_chunks = solo_out(n)[:, k0:k0 + chunks]
                    low_part(out_chunks[:, :, 1, :], relus, out_chunks[:, :, 0, :], flip_lo)

            vocab = tables.shape[0] // TABLES
            dve.wait_ge(idx_in, 16)
            nc.vector.tensor_scalar(idx_wrap[:], idx_raw[:], 0, vocab, ALU.is_lt, ALU.mult).then_inc(idx_steps, 1)
            dve.wait_ge(idx_steps, 1)
            nc.vector.tensor_tensor(idx_wrap[:], idx_raw[:], idx_wrap[:], ALU.add).then_inc(idx_steps, 1)
            dve.wait_ge(idx_steps, 2)
            nc.vector.tensor_scalar(idx_raw[:], idx_wrap[:], 0, vocab - 1, ALU.max, ALU.min).then_inc(idx_steps, 1)
            dve.wait_ge(idx_steps, 3)
            dve.wait_ge(base_done, 1)
            nc.vector.tensor_tensor(rows_of[:], rows_of[:], idx_raw[:], ALU.add).then_inc(idx_steps, 1)
            nc.vector.memset(vT[:, :, :, TABLES + 1:SLOT], 0.0).then_inc(vT_pads, 1)
            nc.vector.memset(pairs[:], 0.0).then_inc(pairs_zero, 1)
            for step in START_ORDER:
                if step[0] == "weights":
                    split_weights(step[1])
                if step[0] == "turn":
                    turn(*step[1:])
                if step[0] == "dots":
                    if step[1:] == (0, 0):
                        dve.wait_ge(pairs_zero, 1)
                    span(step[1], step[2], step[1] % 2, first_use=(step[1] == 0))
                if step[0] == "solo_split":
                    solo_split(step[1])
                if step[0] == "flip":
                    flip(*step[1:])
                if step[0] == "split":
                    split_input(1)

            def run_group(order, g, t):
                for step in order:
                    if step[0] == "turn":
                        turn(t + step[1], step[2])
                    if step[0] == "dots":
                        span(t + step[1], step[2], step[1])
                    if step[0] == "split":
                        split_input(g + 1)
                    if step[0] == "block":
                        top_block(g, step[1])

            with dve.Fori(1, GROUPS - 2) as g:
                run_group(ORDER, g, 2 * g + 2)
            run_group(NEXT_LAST_ORDER, GROUPS - 2, TILES - 2)
            run_group(LAST_ORDER, GROUPS - 1, TILES)


def kernel(**inputs):
    import numpy as np
    import concourse.bacc as bacc
    from concourse.bass_utils import run_bass_kernel_spmd as run

    a = {k.removeprefix("L0_rec_"): np.asarray(v) for k, v in inputs.items()}

    def by_block(v):
        return v.reshape(-1, P).T

    xT = a["r_numerical_input"].reshape(P, TILES, DENSE).transpose(2, 1, 0).reshape(DENSE, B)
    idx = a["r_categorical_inputs"].reshape(P, TILES * TABLES)
    vecs = np.concatenate([by_block(a[k]) for k in ("bb0", "bb1", "bb2", "tb0", "tb1", "tb2", "tb3")]
                          + [by_block(a["tw4"].reshape(-1))], axis=1)
    pair = np.full((3, P), -1)
    for c in range(3):
        for r in range(4):
            j = big_column(c, r)
            pair[c, 32 * r:32 * r + j] = D + j * (j - 1) // 2 + np.arange(j)
    for j, c, at in SMALL_PLACE:
        pair[c, at:at + j] = D + j * (j - 1) // 2 + np.arange(j)
    pair[np.unravel_index(np.argmin(pair), pair.shape)] = TOP_IN - 1
    feature = np.concatenate([np.arange(D), pair.reshape(-1)])
    w0 = np.zeros((feature.size, TOP[0]), a["tw0"].dtype)
    w0[feature >= 0] = a["tw0"].T[feature[feature >= 0]]
    arrays = {
        "xT": xT, "idx": idx, "tables": a["emb_tables"].reshape(-1, D),
        "bw0": a["bw0"].T, "bw1": a["bw1"].T, "bw2": a["bw2"].T,
        "w0": w0, "w1": a["tw1"].T, "w2": a["tw2"].T, "w3": a["tw3"].T,
        "vecs": vecs, "last_bias": a["tb4"].reshape(1, 1),
    }
    arrays = {k: np.ascontiguousarray(v) for k, v in arrays.items()}
    nc = bacc.Bacc("TRN2", target_bir_lowering=False, num_devices=1)
    args = [nc.dram_tensor(k, v.shape, mybir.dt.from_np(v.dtype), kind="ExternalInput").ap()
            for k, v in arrays.items()]
    out = nc.dram_tensor("out", (B, 1), F32, kind="ExternalOutput").ap()
    build(nc, *args, out)
    return run(nc, [arrays], core_ids=[0]).results[0]["out"]
```
